# Optimizing a Trainium2 kernel written in Bass

```python
import numpy as np
import jax
import jax.numpy as jnp

def _softmax(x, axis=-1):
    return jax.nn.softmax(x, axis=axis)

def _gelu(x):
    return jax.nn.gelu(x, approximate=True)

def _silu(x):
    return jax.nn.silu(x)

def _sigmoid(x):
    return jax.nn.sigmoid(x)

def _layernorm(x, axis=-1, eps=1e-05):
    m = jnp.mean(x, axis=axis, keepdims=True)
    v = jnp.var(x, axis=axis, keepdims=True)
    return (x - m) / jnp.sqrt(v + eps)

def _scatter_add(tgt, idx, src, axis=0):
    return tgt.at[idx].add(src)

def _segment_sum(src, seg, n):
    return jax.ops.segment_sum(src, seg, n)
kernel_name = 'mk_flamingo_gated_d1_seqx_r8_f744bf'

def setup_inputs(seed: int=0):
    np.random.seed(seed)
    _w = jnp.asarray

    def _rec_inputs():
        import jax
        import jax.numpy as jnp
        _rk = jax.random.key(seed)
        x = 7.22e-05 + 1 * jax.random.normal(jax.random.fold_in(_rk, 1), (32, 128, 128), jnp.float32)
        _lenS = 128 - jax.random.randint(jax.random.fold_in(_rk, 7), (32,), 0, max(1, 128 // 4) + 1, jnp.int32)
        _lenS2 = 128 - jax.random.randint(jax.random.fold_in(_rk, 8), (32,), 0, max(1, 128 // 4) + 1, jnp.int32)
        _ctx_1024P = jax.random.normal(jax.random.fold_in(_rk, 11), (32, 16, 128), jnp.float32)
        _ctx_1024c = jax.random.dirichlet(jax.random.fold_in(_rk, 511), 0.3 * jnp.ones((16,), jnp.float32), (32, 128))
        _ctx_1024t = jnp.einsum('bsk,bkd->bsd', _ctx_1024c, _ctx_1024P)
        _ctx_1024t = _ctx_1024t * jax.lax.rsqrt(jnp.mean(jnp.square(_ctx_1024t)) + 1e-12) * 0.953939
        ctx_1024 = 4.13588e-05 + 0.999923 * (_ctx_1024t + 0.3 * jax.random.normal(jax.random.fold_in(_rk, 611), (32, 128, 128), jnp.float32))
        _g = jax.random.normal(jax.random.fold_in(_rk, 9001), (2, 1), jnp.float32)
        _g = jnp.sign(_g) * jnp.maximum(jnp.abs(_g), 1.0) + (_g == 0) * 1.0
        g_xattn = _g[0]
        g_ffn = _g[1]
        return (x, ctx_1024, g_xattn, g_ffn)
    x, ctx_1024, g_xattn, g_ffn = _rec_inputs()

    def _L0_xattn_setup():
        import jax, jax.numpy as jnp
        import numpy as np
        D_MODEL = 128
        H = 16
        D_K = D_MODEL // H
        key = jax.random.key(seed)
        ks = jax.random.split(key, 8)
        B, S = (4, 256)
        q = jax.random.normal(ks[0], (B, S, D_MODEL), dtype=jnp.float32)
        k = jax.random.normal(ks[1], (B, S, D_MODEL), dtype=jnp.float32)
        v = jax.random.normal(ks[2], (B, S, D_MODEL), dtype=jnp.float32)
        scale = 1.0 / np.sqrt(D_MODEL)
        W_q = jax.random.normal(ks[3], (H, D_MODEL, D_K), dtype=jnp.float32) * scale
        W_k = jax.random.normal(ks[4], (H, D_MODEL, D_K), dtype=jnp.float32) * scale
        W_v = jax.random.normal(ks[5], (H, D_MODEL, D_K), dtype=jnp.float32) * scale
        W_o = jax.random.normal(ks[6], (D_MODEL, H * D_K), dtype=jnp.float32) * scale
        b_o = jax.random.normal(ks[7], (D_MODEL,), dtype=jnp.float32) * 0.01
        return {'q': q, 'k': k, 'v': v, 'W_q': W_q, 'W_k': W_k, 'W_v': W_v, 'W_o': W_o, 'b_o': b_o}
    _L0_xattn_all = _L0_xattn_setup()
    _L0_xattn_in = {k: v for k, v in _L0_xattn_all.items() if k in ('W_q', 'W_k', 'W_v', 'W_o', 'b_o')}
    del _L0_xattn_all

    def _L0_ffn_setup():
        import jax, jax.numpy as jnp
        import numpy as np
        EMB = 128
        FF = 4 * EMB

        def _ternary(w):
            scale = jnp.maximum(jnp.mean(jnp.abs(w)), 1e-08)
            w_t = jnp.clip(jnp.round(w / scale), -1.0, 1.0)
            return w + jax.lax.stop_gradient(w_t - w)
        key = jax.random.key(seed)
        kx, k1, k2, kb1, kb2 = jax.random.split(key, 5)
        x = jax.random.normal(kx, (4, 256, EMB), dtype=jnp.float32)
        lim1 = 1.0 / np.sqrt(EMB)
        lim2 = 1.0 / np.sqrt(FF)
        W1 = jax.random.uniform(k1, (FF, EMB), jnp.float32, -lim1, lim1)
        b1 = jax.random.uniform(kb1, (FF,), jnp.float32, -lim1, lim1)
        W2 = jax.random.uniform(k2, (EMB, FF), jnp.float32, -lim2, lim2)
        b2 = jax.random.uniform(kb2, (EMB,), jnp.float32, -lim2, lim2)
        return {'x': x, 'W1': W1, 'b1': b1, 'W2': W2, 'b2': b2}
    _L0_ffn_all = _L0_ffn_setup()
    _L0_ffn_in = {k: v for k, v in _L0_ffn_all.items() if k in ('W1', 'b1', 'W2', 'b2')}
    del _L0_ffn_all
    return {'x': x, 'ctx_1024': ctx_1024, 'g_xattn': g_xattn, 'g_ffn': g_ffn, 'L0_xattn_W_q': _L0_xattn_in['W_q'], 'L0_xattn_W_k': _L0_xattn_in['W_k'], 'L0_xattn_W_v': _L0_xattn_in['W_v'], 'L0_xattn_W_o': _L0_xattn_in['W_o'], 'L0_xattn_b_o': _L0_xattn_in['b_o'], 'L0_ffn_W1': _L0_ffn_in['W1'], 'L0_ffn_b1': _L0_ffn_in['b1'], 'L0_ffn_W2': _L0_ffn_in['W2'], 'L0_ffn_b2': _L0_ffn_in['b2']}

def reference(x, ctx_1024, g_xattn, g_ffn, L0_xattn_W_q, L0_xattn_W_k, L0_xattn_W_v, L0_xattn_W_o, L0_xattn_b_o, L0_ffn_W1, L0_ffn_b1, L0_ffn_W2, L0_ffn_b2):
    import jax
    import jax.numpy as jnp

    def _L0_xattn_ref(q, k, v, W_q, W_k, W_v, W_o, b_o):
        import jax, jax.numpy as jnp
        import numpy as np
        D_MODEL = 128
        H = 16
        D_K = D_MODEL // H
        qh = jnp.einsum('bsd,hdk->hbsk', q, W_q)
        kh = jnp.einsum('bsd,hdk->hbsk', k, W_k)
        vh = jnp.einsum('bsd,hdk->hbsk', v, W_v)
        scores = jnp.einsum('hbsk,hbtk->hbst', qh, kh) / jnp.sqrt(jnp.asarray(D_K, qh.dtype))
        attn = jax.nn.softmax(scores, axis=-1)
        out = jnp.einsum('hbst,hbtk->hbsk', attn, vh)
        out = jnp.transpose(out, (1, 2, 0, 3)).reshape(q.shape[0], q.shape[1], H * D_K)
        return out @ W_o.T + b_o

    def _L0_ffn_ref(x, W1, b1, W2, b2):
        import jax, jax.numpy as jnp
        import numpy as np
        EMB = 128
        FF = 4 * EMB

        def _ternary(w):
            scale = jnp.maximum(jnp.mean(jnp.abs(w)), 1e-08)
            w_t = jnp.clip(jnp.round(w / scale), -1.0, 1.0)
            return w + jax.lax.stop_gradient(w_t - w)
        h = jnp.einsum('bsd,fd->bsf', x, _ternary(W1)) + b1
        h = jax.nn.gelu(h, approximate=False)
        out = jnp.einsum('bsf,df->bsd', h, _ternary(W2)) + b2
        return out
    x = x + jnp.tanh(g_xattn[0]) * _L0_xattn_ref(_layernorm(x, axis=-1), ctx_1024, ctx_1024, L0_xattn_W_q, L0_xattn_W_k, L0_xattn_W_v, L0_xattn_W_o, L0_xattn_b_o)
    x = x + jnp.tanh(g_ffn[0]) * _L0_ffn_ref(_layernorm(x, axis=-1), L0_ffn_W1, L0_ffn_b1, L0_ffn_W2, L0_ffn_b2)
    return x

_drawn_inputs = setup_inputs


def setup_inputs(seed=0):
    import zlib

    import numpy as np

    out = dict(_drawn_inputs(seed))
    spreads = {}
    factors = {'L0_xattn_b_o': 7.742, 'L0_ffn_b1': 8.0, 'L0_ffn_b2': 200.0}
    for name, (base, spread) in spreads.items():
        noise = np.random.default_rng([zlib.crc32(name.encode()), seed]).standard_normal(out[name].shape)
        drawn = base * np.exp(spread * noise) if base else spread * noise
        out[name] = jnp.asarray(drawn.astype(out[name].dtype))
    for name, factor in factors.items():
        out[name] = (out[name] * factor).astype(out[name].dtype)
    return out
```

```python
from contextlib import ExitStack

import concourse.bass as bass
from concourse import mybir

P = 128
D = 128
B = 32
H = 16
DK = D // H
FF = 4 * D
FC = FF // P
NPART = 3
PROD = NPART * NPART * DK
MROW = 96
QUAD = 4
UNITS = H // QUAD
PAIRS = H // 2
VW = 2 * DK + 1
BODY = 6
LEAD, LAG = 5, 4
RING = 6
FIRST = LAG + 1
LOOPS = (B - LEAD - 1 - FIRST) // BODY
LAST = FIRST + LOOPS * BODY
GROUP = 4
GROUPS = B // GROUP
XFIRST, XNEXT = 2, 8
LN_EPS = 1e-5

ALU = mybir.AluOpType
ACT = mybir.ActivationFunctionType
AX = mybir.AxisListType
F32 = mybir.dt.float32
BF16 = mybir.dt.bfloat16
assert BODY % RING == 0


def entry(T, m):
    return m if isinstance(T, int) else T * BODY + m


def live(T, m):
    return not isinstance(T, int) or 0 <= m < B


def steps(T, m, per=1, part=None):
    part = per if part is None else part
    if isinstance(T, int):
        return 0 if m < 0 else per * m + part if m < B else per * B
    assert per * m + part > 0
    return T * (BODY * per) + (per * m + part)


def after(eng, sem, T, m, per=1, part=None):
    value = steps(T, m, per, part)
    if not isinstance(value, int) or value > 0:
        eng.wait_ge(sem, value)


def transfers(T, m, ring, per=1):
    if isinstance(T, int):
        return 0 if m < 0 else 16 * per * (m // ring + 1)
    assert m // ring + 1 > 0
    return T * (16 * per * (BODY // ring)) + 16 * per * (m // ring + 1)


def landed(eng, sems, T, m, per=1):
    value = transfers(T, m, len(sems), per)
    if not isinstance(value, int) or value > 0:
        eng.wait_ge(sems[m % len(sems)], value)


def periods(eng, period):
    for n in range(-LEAD - 1, FIRST):
        period(0, n)
    with eng.Fori(0, LOOPS) as T:
        for n in range(FIRST, FIRST + BODY):
            period(T, n)
    for n in range(LAST, B + LAG):
        period(0, n)


def build(nc, x, ctxT, g_xattn, g_ffn, Wq, Wk, Wv, WoT, b_o, W1T, b1, W2T, b2, out, part_dram):
    with ExitStack() as es:
        def sb(name, shape, dt=F32):
            return es.enter_context(nc.sbuf_tensor(name, shape, dt))

        def ps(name, shape, dt=F32):
            return es.enter_context(nc.psum_tensor(name, shape, dt))

        def sem(name):
            return es.enter_context(nc.semaphore(name))

        xs = sb("xs", [P, B, D])
        ctx_sb = sb("ctx_sb", [D, RING, P])
        x2T = sb("x2T", [D, B * P])
        wq, wk, wv = sb("wq", [D, D]), sb("wk", [D, D]), sb("wv", [D, D])
        wo = sb("wo", [D, D])
        w1, w2 = sb("w1", [D, FF]), sb("w2", [P, FC * D])
        tern = sb("tern", [P, 2, FF])
        wsum = sb("wsum", [P, 2])
        wscale = sb("wscale", [P, 3, 2])
        b1_sb = sb("b1_sb", [P, FC])
        gate = sb("gate", [P, 2])
        tgate = sb("tgate", [P, 2])
        brow = sb("brow", [1, 2 * D])
        brest = sb("brest", [1, 2, 2 * D])
        bsplit = sb("bsplit", [1, NPART, 2 * D], BF16)
        bparts = sb("bparts", [NPART, 2 * D], BF16)
        ones3 = sb("ones3", [NPART, P], BF16)
        ones = sb("ones", [P, P])
        ident = sb("ident", [P, P])
        identb = sb("identb", [P, P], BF16)
        mhalf = sb("mhalf", [P, 1])

        st1 = sb("st1", [P, 2, 6])
        mv1 = sb("mv1", [P, 2, 2])
        nv1 = sb("nv1", [P, 2, 2])
        rs1 = sb("rs1", [P, 2])
        xh = sb("xh", [P, 2, D])
        xhT = sb("xhT", [D, 2, P])
        parts = sb("parts", [P, 2, 2, NPART, P], BF16)
        rest = sb("rest", [P, 2, 2, P])
        qa = sb("qa", [P, RING, H, P], BF16)
        ka = sb("ka", [P, RING, H, P], BF16)
        va = sb("va", [P, RING, PAIRS, VW])
        nmax = sb("nmax", [P, 2, H])
        nrest = sb("nrest", [P, 2, 2, H])
        npart = sb("npart", [P, 2, P // H, H], BF16)
        zeros = sb("zeros", [P, 2 * P])
        nT = sb("nT", [NPART * H, 2, P], BF16)
        probs = sb("probs", [P, 2, UNITS, QUAD * P])
        oT = sb("oT", [P, 2, 4 * P])
        rden = sb("rden", [P, 2, H])
        on = sb("on", [P, 2, D])
        onT = sb("onT", [D, 2, P])
        x2 = sb("x2", [P, 2, D])
        st2 = sb("st2", [P, 2, 6])
        mv2 = sb("mv2", [P, 2, 2])
        nv2 = sb("nv2", [P, 2, 2])
        rs2 = sb("rs2", [P, 2])
        xh2 = sb("xh2", [P, 2, D])
        hT = sb("hT", [P, 2, FC, GROUP * P])
        res = sb("res", [P, 2, GROUP, D])

        pS = [ps(f"pS{i}", [P, QUAD * P]) for i in range(2)]
        pT = [ps(f"pT{i}", [P, QUAD * P]) for i in range(2)]
        pO = ps("pO", [P, 4 * P])
        pR = ps("pR", [P, 4 * P])
        pA = ps("pA", [P, 4 * P])
        pB = ps("pB", [P, 4 * P])
        pAb = pA[:, :].bitcast(BF16)
        hbank = [pS[0], pS[1], pT[0], pT[1]]
        ybank = [pO, pR]

        x_in = [sem(f"x_in{i}") for i in range(3)]
        ctx_in = [sem(f"ctx_in{i}") for i in range(RING)]
        proj_in, w_in, small_in, bias_in = sem("proj_in"), sem("w_in"), sem("small_in"), sem("bias_in")
        parts_stored = [sem(f"parts_stored{i}") for i in range(3)]
        aug_loaded = [sem(f"aug_loaded{i}") for i in range(RING)]
        max_loaded = [sem(f"max_loaded{i}") for i in range(2)]
        out_stored = [sem(f"out_stored{i}") for i in range(2)]
        ident_zero, ident_made, identb_made, consts_made = (
            sem("ident_zero"), sem("ident_made"), sem("identb_made"), sem("consts_made"))
        pool_zero, dve_zero, krows_made = sem("pool_zero"), sem("dve_zero"), sem("krows_made")
        gates_made, bias_step, bias_split = sem("gates_made"), sem("bias_step"), sem("bias_split")
        wsum_made, wtotal_made, wstep, w_made = sem("wsum_made"), sem("wtotal_made"), sem("wstep"), sem("w_made")
        scored, keyed, pv_done = sem("scored"), sem("keyed"), sem("pv_done")
        o_turned, on_turned, wo_done = sem("o_turned"), sem("on_turned"), sem("wo_done")
        max_turned, xh_turned, projected, xh2_turned = sem("max_turned"), sem("xh_turned"), sem("projected"), sem("xh2_turned")
        reduced, bn1_done, mv1_done, stats1 = sem("reduced"), sem("bn1_done"), sem("mv1_done"), sem("stats1")
        xh_made, rest_made, rden_made, on_made = sem("xh_made"), sem("rest_made"), sem("rden_made"), sem("on_made")
        x2_made, bn2_done, mv2_done, stats2 = sem("x2_made"), sem("bn2_done"), sem("mv2_done"), sem("stats2")
        exped, max_copied, o_copied, on_copied = sem("exped"), sem("max_copied"), sem("o_copied"), sem("on_copied")
        xh_copied, v_copied, first_made, x2_kept, xh2_copied = (
            sem("xh_copied"), sem("v_copied"), sem("first_made"), sem("x2_kept"), sem("xh2_copied"))
        nsplit, max_split, rs1_made, mid_made, parts_made, rs2_made, xh2_made = (
            sem("nsplit"), sem("max_split"), sem("rs1_made"), sem("mid_made"), sem("parts_made"), sem("rs2_made"),
            sem("xh2_made"))
        hidden, gelued, y_done, res_made = sem("hidden"), sem("gelued"), sem("y_done"), sem("res_made")

        x_dram = x.rearrange("b s d -> s b d")
        out_dram = out.rearrange("(g b) s d -> g s b d", b=GROUP)
        block = es.enter_context(nc.Block())

        @block.sync
        def _(sp):
            def load_context(T, m):
                after(sp, projected, T, m - RING)
                sp.dma_start(ctx_sb[:, m % RING], ctxT[:, entry(T, m), :]).then_inc(ctx_in[m % RING], 16)

            edges = [0, XFIRST, XNEXT, B]
            for i in range(3):
                sp.dma_start(xs[:, edges[i]:edges[i + 1], :], x_dram[:, edges[i]:edges[i + 1], :]).then_inc(x_in[i], 16)
                if i == 0:
                    load_context(0, 0)
            sp.wait_ge(bias_split, 1)
            sp.dma_start(bparts[:, :], bsplit[:, :, :]).then_inc(bias_in, 16)
            sp.wait_ge(pool_zero, 1)
            sp.wait_ge(dve_zero, 1)

            def period(T, n):
                if live(T, n + LEAD + 1) and not (isinstance(T, int) and n == -LEAD - 1):
                    load_context(T, n + LEAD + 1)
                m = n + LEAD - 1
                if live(T, m):
                    slot, dslot = m % 2, m % 3
                    after(sp, parts_made, T, m)
                    sp.dma_start(part_dram[dslot].rearrange("w i r s -> r (w i) s"),
                                 parts[:, slot].rearrange("p w i s -> p (w i) s")).then_inc(parts_stored[dslot], 16)
                    landed(sp, parts_stored, T, m)
                    qsrc = part_dram[dslot, 0].rearrange("i (k h) s -> (i k) (h s)", k=DK)
                    ksrc = part_dram[dslot, 1].rearrange("j (k h) s -> k j (h s)", k=DK)
                    sp.dma_start(qa[0:PROD, m % RING], qsrc.unsqueeze(1).to_broadcast([NPART * DK, NPART, H * P])
                                 ).then_inc(aug_loaded[m % RING], 16)
                    for i in range(NPART):
                        rows = slice(i * NPART * DK, (i + 1) * NPART * DK)
                        sp.dma_start(ka[rows, m % RING], ksrc).then_inc(aug_loaded[m % RING], 16)

            periods(sp, period)

            def store(T, g):
                group = g if isinstance(T, int) else T * 2 + g
                sp.wait_ge(res_made, group + 1)
                sp.dma_start(out_dram[group], res[:, g % 2]).then_inc(out_stored[g % 2], 16)

            with sp.Fori(0, GROUPS // 2) as T:
                for g in range(2):
                    store(T, g)
            for g in range(2):
                sp.wait_ge(out_stored[g], 16 * (GROUPS // 2))

        @block.gpsimd
        def _(pool):
            pool.memset(ident[:, :], 0.0).then_inc(ident_zero, 1)
            pool.wait_ge(ident_zero, 1)
            pool.affine_select(out=ident[:, :], in_=ident[:, :], compare_op=ALU.not_equal, fill=1.0, base=0,
                               pattern=[[-1, P]], channel_multiplier=1).then_inc(ident_made, 1)
            pool.memset(zeros[:, :], 0.0).then_inc(consts_made, 1)
            pool.memset(npart[:, :, :, :], 0.0).then_inc(consts_made, 1)
            pool.memset(mhalf[:, :], -0.5).then_inc(consts_made, 1)
            pool.wait_ge(consts_made, 3)
            pool.memset(qa[64:P].rearrange("p r h s -> p (r h s)").bitcast(F32), 0.0).then_inc(pool_zero, 1)
            pool.wait_ge(pool_zero, 1)

            def period(T, n):
                m = n + 1
                if live(T, m):
                    s = m % 2
                    after(pool, reduced, T, m, UNITS)
                    after(pool, max_turned, T, m - 2)
                    pool.tensor_tensor(npart[:, s, 0], nmax[:, s], zeros[:, 0:H], ALU.add).then_inc(nsplit, 1)
                    after(pool, nsplit, T, m, 4, 1)
                    pool.tensor_tensor(nrest[:, s, 0], nmax[:, s], npart[:, s, 0], ALU.subtract).then_inc(nsplit, 1)
                    after(pool, nsplit, T, m, 4, 2)
                    pool.tensor_tensor(npart[:, s, 1], nrest[:, s, 0], zeros[:, 0:H], ALU.add).then_inc(nsplit, 1)
                    after(pool, nsplit, T, m, 4, 3)
                    pool.tensor_tensor(npart[:, s, 2], nrest[:, s, 0], npart[:, s, 1], ALU.subtract
                                       ).then_inc(nsplit, 1)
                m = n + LEAD - 1
                s = m % 2
                if live(T, m):
                    after(pool, rest_made, T, m)
                    landed(pool, parts_stored, T, m - 2)
                    pool.tensor_tensor(parts[:, s, :, 1], rest[:, s], zeros[:, :].rearrange("p (w s) -> p w s", w=2),
                                       ALU.add).then_inc(mid_made, 1)
                k = n - 3
                if live(T, k):
                    after(pool, stats2, T, k)
                    pool.tensor_tensor(rs2[:, k % 2:k % 2 + 1], nv2[:, k % 2, 1:2], mhalf[:, :], ALU.pow
                                       ).then_inc(rs2_made, 1)
                    after(pool, rs2_made, T, k)
                if live(T, m):
                    after(pool, mid_made, T, m)
                    pool.tensor_tensor(parts[:, s, :, 2], rest[:, s], parts[:, s, :, 1], ALU.subtract
                                       ).then_inc(parts_made, 1)
                if live(T, k):
                    pool.tensor_scalar(xh2[:, k % 2], x2[:, k % 2], nv2[:, k % 2, 0:1], rs2[:, k % 2:k % 2 + 1],
                                       ALU.add, ALU.mult).then_inc(xh2_made, 1)
                m = n + LEAD + 1
                if live(T, m):
                    s = m % 2
                    after(pool, stats1, T, m)
                    pool.tensor_tensor(rs1[:, s:s + 1], nv1[:, s, 1:2], mhalf[:, :], ALU.pow).then_inc(rs1_made, 1)

            periods(pool, period)

        @block.scalar
        def _(act):
            for dst, src in ((wq, Wq), (wk, Wk), (wv, Wv), (wo, WoT)):
                act.dma_start(dst[:, :], src).then_inc(proj_in, 16)
            act.dma_start(gate[:, 0:1], g_xattn.partition_broadcast(P)).then_inc(small_in, 16)
            act.dma_start(gate[:, 1:2], g_ffn.partition_broadcast(P)).then_inc(small_in, 16)
            act.dma_start(brow[:, 0:D], b_o).then_inc(small_in, 16)
            act.dma_start(brow[:, D:2 * D], b2).then_inc(small_in, 16)
            act.dma_start(b1_sb[:, :], b1).then_inc(small_in, 16)
            act.dma_start(w1[:, :], W1T).then_inc(w_in, 16)
            act.dma_start(w2[:, :].rearrange("p (c d) -> p c d", c=FC), W2T).then_inc(w_in, 16)
            act.wait_ge(small_in, 16 * 5)
            act.activation(tgate[:, :], gate[:, :], ACT.Tanh).then_inc(gates_made, 1)
            act.wait_ge(dve_zero, 1)
            act.wait_ge(pool_zero, 1)

            def exp(T, n, u):
                if not live(T, n):
                    return
                after(act, keyed, T, n, UNITS, u + 1)
                after(act, pv_done, T, n - 2, 2, u // 2 + 1)
                act.activation(probs[:, n % 2, u], pT[u % 2][:, :], ACT.Exp, scale=float(DK) ** -0.5
                               ).then_inc(exped, 1)

            def period(T, n):
                exp(T, n - 1, 2)
                m = n - 2
                if live(T, m):
                    after(act, pv_done, T, m, 2)
                    after(act, o_turned, T, m - 2)
                    act.copy(oT[:, m % 2], pO[:, :]).then_inc(o_copied, 1)
                exp(T, n - 1, 3)
                m = n + 1
                if live(T, m):
                    s = m % 2
                    after(act, max_turned, T, m)
                    landed(act, max_loaded, T, m - 2)
                    act.copy(nT[:, s], pAb[0:NPART * H, 0:P]).then_inc(max_copied, 1)
                    after(act, max_copied, T, m)
                    act.dma_start(qa[MROW:MROW + NPART, m % RING], nT[:, s]).then_inc(max_loaded[s], 16)
                exp(T, n, 0)
                m = n - 4
                if live(T, m):
                    after(act, xh2_turned, T, m)
                    e = entry(T, m)
                    act.copy(x2T[:, bass.ds(e * P, P)], pB[:, 0:P]).then_inc(xh2_copied, 1)
                m = n + LEAD
                if live(T, m):
                    after(act, xh_turned, T, m)
                    act.copy(xhT[:, m % 2], pA[:, 0:P]).then_inc(xh_copied, 1)
                m = n - 3
                if live(T, m):
                    after(act, x2_made, T, m)
                    act.copy(xs[:, entry(T, m), :], x2[:, m % 2]).then_inc(x2_kept, 1)
                exp(T, n, 1)
                m = n - 2
                if live(T, m):
                    after(act, on_turned, T, m)
                    act.copy(onT[:, m % 2], pB[:, 0:P]).then_inc(on_copied, 1)
                m = n + LEAD
                if live(T, m):
                    after(act, projected, T, m)
                    stored_before(act, T, m)
                    act.copy(parts[:, m % 2, :, 0], pA[:, 0:2 * P].rearrange("p (w s) -> p w s", w=2)
                             ).then_inc(first_made, 1)
                    after(act, pv_done, T, m - RING, 2)
                    vdst = va[:, m % RING].rearrange("p (b j) w -> p b j w", b=2)
                    vsrc = pA[:, 2 * P:3 * P].rearrange("p (b r j k) -> p b r j k", b=2, r=2, j=4)
                    for r in range(2):
                        act.copy(vdst[:, :, :, r * DK:(r + 1) * DK], vsrc[:, :, r]).then_inc(v_copied, 1)

            def stored_before(eng, T, m):
                landed(eng, parts_stored, T, m - 2)

            periods(act, period)

            def gelu(T, g):
                group = g if isinstance(T, int) else T * 2 + g
                for c in range(FC):
                    act.wait_ge(hidden, group * FC + (c + 1))
                    if not isinstance(T, int) or g >= 2:
                        act.wait_ge(y_done, group - 1)
                    act.activation(hT[:, g % 2, c], hbank[c][:, :], ACT.Gelu, bias=b1_sb[:, c:c + 1]
                                   ).then_inc(gelued, 1)

            gelu(0, 0)
            gelu(0, 1)
            with act.Fori(1, GROUPS // 2) as T:
                for g in range(2):
                    gelu(T, g)

        @block.vector
        def _(dve):
            dve.memset(va[:, :, :, :], 1.0)
            dve.memset(pO[:, :], 0.0)
            dve.memset(ones3[:, :], 1.0)
            dve.memset(ones[:, :], 1.0)
            dve.memset(ka[64:P].rearrange("p r h s -> p (r h s)").bitcast(F32), 0.0).then_inc(krows_made, 1)
            dve.wait_ge(krows_made, 1)
            dve.memset(ka[MROW:MROW + NPART], 1.0).then_inc(dve_zero, 1)
            dve.wait_ge(ident_made, 1)
            dve.tensor_copy(identb[:, :], ident[:, :]).then_inc(identb_made, 1)

            def split_biases():
                dve.wait_ge(small_in, 16 * 5)
                dve.tensor_copy(bsplit[:, 0], brow[:, :]).then_inc(bias_step, 1)
                dve.wait_ge(bias_step, 1)
                dve.tensor_tensor(brest[:, 0], brow[:, :], bsplit[:, 0], ALU.subtract).then_inc(bias_step, 1)
                dve.wait_ge(bias_step, 2)
                dve.tensor_copy(bsplit[:, 1], brest[:, 0]).then_inc(bias_step, 1)
                dve.wait_ge(bias_step, 3)
                dve.tensor_tensor(bsplit[:, 2], brest[:, 0], bsplit[:, 1], ALU.subtract).then_inc(bias_split, 1)

            def weight_sums():
                dve.wait_ge(w_in, 32)
                for i, w in enumerate((w1, w2)):
                    ins = dve.tensor_reduce(wsum[:, i:i + 1], w[:, :], AX.X, ALU.add, apply_absolute_value=True)
                ins.then_inc(wsum_made, 1)

            def ternary():
                dve.wait_ge(wtotal_made, 1)
                dve.tensor_scalar(wscale[:, 0], pR[:, 0:2], 1.0 / (D * FF), 1e-8, ALU.mult, ALU.max).then_inc(wstep, 1)
                dve.wait_ge(wstep, 1)
                dve.tensor_scalar(wscale[:, 1], wscale[:, 0], 0.5, None, ALU.mult).then_inc(wstep, 1)
                dve.tensor_scalar(wscale[:, 2], wscale[:, 0], -0.5, None, ALU.mult).then_inc(wstep, 1)
                dve.wait_ge(wstep, 3)
                for i, w in enumerate((w1, w2)):
                    step = 3 + 3 * i
                    dve.tensor_scalar(tern[:, 0], w[:, :], wscale[:, 1, i:i + 1], None, ALU.is_gt).then_inc(wstep, 1)
                    dve.wait_ge(wstep, step + 1)
                    dve.scalar_tensor_tensor(out=tern[:, 1], in0=w[:, :], scalar=wscale[:, 2, i:i + 1],
                                             in1=tern[:, 0], op0=ALU.is_lt, op1=ALU.subtract).then_inc(wstep, 1)
                    dve.wait_ge(wstep, step + 2)
                    dve.tensor_tensor(tern[:, 0], w[:, :], tern[:, 1], ALU.add).then_inc(wstep, 1)
                    dve.wait_ge(wstep, step + 3)
                    dve.tensor_tensor(w[:, :], w[:, :], tern[:, 0], ALU.subtract).then_inc(w_made, 1)
                    dve.wait_ge(w_made, i + 1)

            def row_max(T, m, u):
                if not live(T, m):
                    return
                after(dve, scored, T, m, UNITS, u + 1)
                if u == 0:
                    after(dve, nsplit, T, m - 2, 4)
                dve.tensor_reduce(nmax[:, m % 2, u * QUAD:(u + 1) * QUAD],
                                  pS[u % 2][:, :].rearrange("p (h s) -> p h s", h=QUAD), AX.X, ALU.max,
                                  negate=True).then_inc(reduced, 1)

            def aggregate(T, m, st, mv, nv, agg, done):
                s = m % 2
                dve.bn_aggr(mv[:, s], st[:, s]).then_inc(agg, 1)
                after(dve, agg, T, m)
                dve.tensor_scalar(nv[:, s, 0:1], mv[:, s, 0:1], -1.0, None, ALU.mult)
                dve.tensor_scalar(nv[:, s, 1:2], mv[:, s, 1:2], LN_EPS, None, ALU.add).then_inc(done, 1)

            def period(T, n):
                row_max(T, n + 2, 0)
                m = n + LEAD - 1
                if live(T, m):
                    s = m % 2
                    after(dve, first_made, T, m)
                    after(dve, v_copied, T, m, 2)
                    after(dve, parts_made, T, m - 2)
                    dve.tensor_tensor(rest[:, s], pA[:, 0:2 * P].rearrange("p (w s) -> p w s", w=2),
                                      parts[:, s, :, 0], ALU.subtract).then_inc(rest_made, 1)
                row_max(T, n + 2, 1)
                m = n + LEAD
                if live(T, m):
                    after(dve, rs1_made, T, m)
                    after(dve, xh_turned, T, m - 2)
                    dve.tensor_scalar(xh[:, m % 2], xs[:, entry(T, m), :], nv1[:, m % 2, 0:1], rs1[:, m % 2:m % 2 + 1],
                                      ALU.add, ALU.mult).then_inc(xh_made, 1)
                m = n - 3
                if live(T, m):
                    s = m % 2
                    after(dve, wo_done, T, m)
                    after(dve, xh2_made, T, m - 2)
                    after(dve, x2_kept, T, m - 2)
                    dve.scalar_tensor_tensor(out=x2[:, s], in0=pB[:, 0:P], scalar=tgate[:, 0:1],
                                             in1=xs[:, entry(T, m), :], op0=ALU.mult, op1=ALU.add).then_inc(x2_made, 1)
                    after(dve, x2_made, T, m)
                    dve.bn_stats(st2[:, s], x2[:, s]).then_inc(bn2_done, 1)
                    after(dve, bn2_done, T, m)
                row_max(T, n + 2, 2)
                if live(T, m):
                    aggregate(T, m, st2, mv2, nv2, mv2_done, stats2)
                m = n - 2
                if live(T, m):
                    s = m % 2
                    after(dve, o_turned, T, m)
                    for b in range(2):
                        den = pR[:, b * 2 * P + 2 * DK:b * 2 * P + 2 * DK + 2 * (P - DK)]
                        den = den.rearrange("p (r c) -> p r c", r=2)[:, :, 0:P - DK]
                        den = den[:, :, 0:97:32]
                        dve.reciprocal(rden[:, s, b * 8:(b + 1) * 8].rearrange("p (r j) -> p r j", r=2), den
                                       ).then_inc(rden_made, 1)
                    after(dve, rden_made, T, m, 2)
                    dve.tensor_tensor(on[:, s].rearrange("p (h k) -> p h k", h=H),
                                      pR[:, :].rearrange("p (h c) -> p h c", h=H)[:, :, 0:DK],
                                      rden[:, s].unsqueeze(2).to_broadcast([P, H, DK]), ALU.mult
                                      ).then_inc(on_made, 1)
                m = n + LEAD + 1
                if live(T, m):
                    if isinstance(T, int) and m in (0, XFIRST, XNEXT):
                        dve.wait_ge(x_in[(0, XFIRST, XNEXT).index(m)], 16)
                    dve.bn_stats(st1[:, m % 2], xs[:, entry(T, m), :]).then_inc(bn1_done, 1)
                    after(dve, bn1_done, T, m)
                row_max(T, n + 2, 3)
                if live(T, m):
                    aggregate(T, m, st1, mv1, nv1, mv1_done, stats1)
                if isinstance(T, int) and n == -4:
                    split_biases()
                    weight_sums()
                if isinstance(T, int) and n == -3:
                    dve.wait_ge(gates_made, 1)
                    ternary()

            periods(dve, period)

            def residual(T, g):
                group = g if isinstance(T, int) else T * 2 + g
                dve.wait_ge(y_done, group + 1)
                if not isinstance(T, int):
                    dve.wait_ge(out_stored[g], T * 16)
                dve.scalar_tensor_tensor(out=res[:, g], in0=ybank[g][:, :].rearrange("p (b d) -> p b d", b=GROUP),
                                         scalar=tgate[:, 1:2], in1=xs[:, bass.ds(group * GROUP, GROUP), :],
                                         op0=ALU.mult, op1=ALU.add).then_inc(res_made, 1)

            dve.wait_ge(x2_kept, B)
            residual(0, 0)
            residual(0, 1)
            with dve.Fori(1, GROUPS // 2) as T:
                for g in range(2):
                    residual(T, g)

        @block.tensor
        def _(pe):
            pe.wait_ge(ident_made, 1)
            pe.wait_ge(identb_made, 1)
            pe.wait_ge(consts_made, 3)
            pe.wait_ge(dve_zero, 1)
            pe.wait_ge(proj_in, 16 * 4)

            def scores(T, n, u):
                if not live(T, n):
                    return
                if u == 0:
                    landed(pe, aug_loaded, T, n, 1 + NPART)
                after(pe, reduced, T, n if u >= 2 else n - 1, UNITS, (u - 2) % UNITS + 1)
                for j in range(QUAD):
                    h = u * QUAD + j
                    mm = pe.matmul(pS[u % 2][:, j * P:(j + 1) * P], qa[0:MROW, n % RING, h], ka[0:MROW, n % RING, h],
                                   start=True, stop=True)
                mm.then_inc(scored, 1)

            def keyed_scores(T, n, u):
                if not live(T, n):
                    return
                if u == 0:
                    landed(pe, max_loaded, T, n)
                after(pe, exped, T, n if u >= 2 else n - 1, UNITS, (u - 2) % UNITS + 1)
                for j in range(QUAD):
                    h = u * QUAD + j
                    mm = pe.matmul(pT[u % 2][:, j * P:(j + 1) * P], ka[:, n % RING, h], qa[:, n % RING, h],
                                   start=True, stop=True)
                mm.then_inc(keyed, 1)

            def probs_v(T, n, b):
                if not live(T, n):
                    return
                after(pe, exped, T, n, UNITS, 2 * b + 2)
                if b == 0:
                    after(pe, v_copied, T, n, 2)
                    after(pe, o_copied, T, n - 1)
                for j in range(4):
                    pr = probs[:, n % 2, 2 * b:2 * b + 2, j * P:(j + 1) * P]
                    mm = pe.matmul(pO[32 * j:32 * j + VW, b * 2 * P:(b + 1) * 2 * P].rearrange("p (r s) -> p r s", r=2),
                                   va[:, n % RING, 4 * b + j], pr, start=True, stop=True)
                mm.then_inc(pv_done, 1)

            def turn_o(T, n):
                if not live(T, n):
                    return
                after(pe, o_copied, T, n)
                after(pe, on_made, T, n - 1)
                for b in range(2):
                    for r in range(2):
                        at = b * 2 * P + r * (P - DK)
                        mm = pe.transpose(pR[:, at:at + P], oT[:, n % 2, (2 * b + r) * P:(2 * b + r + 1) * P], ident[:, :])
                mm.then_inc(o_turned, 1)

            def turn_on(T, n):
                if not live(T, n):
                    return
                after(pe, on_made, T, n)
                after(pe, xh2_copied, T, n - 2)
                pe.transpose(pB[:, 0:P], on[:, n % 2], ident[:, :]).then_inc(on_turned, 1)

            def project_out(T, n):
                if not live(T, n):
                    return
                after(pe, on_copied, T, n)
                if isinstance(T, int) and n == 0:
                    pe.wait_ge(bias_in, 16)
                pe.matmul(pB[:, 0:P], onT[:, n % 2], wo[:, :], start=True, stop=False)
                pe.matmul(pB[:, 0:P], ones3[:, :], bparts[:, 0:D], start=False, stop=True).then_inc(wo_done, 1)

            def turn_xh2(T, n):
                if not live(T, n):
                    return
                after(pe, xh2_made, T, n)
                after(pe, x2_made, T, n + 1)
                after(pe, xh2_copied, T, n - 1)
                pe.transpose(pB[:, 0:P], xh2[:, n % 2], ident[:, :]).then_inc(xh2_turned, 1)

            def turn_max(T, n):
                if not live(T, n):
                    return
                after(pe, nsplit, T, n, 4)
                after(pe, rest_made, T, n + 3)
                after(pe, max_copied, T, n - 1)
                pe.transpose(pAb[:, 0:P], npart[:, n % 2].rearrange("p i h -> p (i h)"), identb[:, :]
                             ).then_inc(max_turned, 1)

            def turn_xh(T, n):
                if not live(T, n):
                    return
                after(pe, xh_made, T, n)
                after(pe, rest_made, T, n - 1)
                after(pe, max_copied, T, n - 4)
                pe.transpose(pA[:, 0:P], xh[:, n % 2], ident[:, :]).then_inc(xh_turned, 1)

            def project(T, n):
                if not live(T, n):
                    return
                after(pe, xh_copied, T, n)
                landed(pe, ctx_in, T, n)
                ctx_n = ctx_sb[:, n % RING]
                pe.matmul(pA[:, 0:P], wq[:, :], xhT[:, n % 2], start=True, stop=True)
                pe.matmul(pA[:, P:2 * P], wk[:, :], ctx_n, start=True, stop=True)
                pe.matmul(pA[:, 2 * P:3 * P], ctx_n, wv[:, :], start=True, stop=True).then_inc(projected, 1)

            def period(T, n):
                scores(T, n + 2, 0)
                keyed_scores(T, n - 1, 2)
                project_out(T, n - 3)
                scores(T, n + 2, 1)
                keyed_scores(T, n - 1, 3)
                probs_v(T, n - 1, 0)
                turn_o(T, n - 2)
                turn_max(T, n + 1)
                scores(T, n + 2, 2)
                keyed_scores(T, n, 0)
                turn_xh2(T, n - 4)
                turn_xh(T, n + LEAD)
                scores(T, n + 2, 3)
                keyed_scores(T, n, 1)
                turn_on(T, n - 2)
                probs_v(T, n - 1, 1)
                project(T, n + LEAD)
                if isinstance(T, int) and n == -4:
                    pe.wait_ge(wsum_made, 1)
                    pe.matmul(pR[:, 0:2], ones[:, :], wsum[:, :], start=True, stop=True).then_inc(wtotal_made, 1)

            periods(pe, period)

            def up(T, g):
                group = g if isinstance(T, int) else T * 2 + g
                if isinstance(T, int) and g == 0:
                    pe.wait_ge(w_made, 2)
                    pe.wait_ge(reduced, B * UNITS)
                    pe.wait_ge(exped, B * UNITS)
                    pe.wait_ge(xh2_copied, B)
                    pe.wait_ge(on_made, B)
                for c in range(FC):
                    if not isinstance(T, int) or g >= 1:
                        pe.wait_ge(gelued, (group - 1) * FC + (c + 1))
                    pe.matmul(hbank[c][:, :], w1[:, c * P:(c + 1) * P], x2T[:, bass.ds(group * GROUP * P, GROUP * P)],
                              start=True, stop=True).then_inc(hidden, 1)

            def down(T, g):
                group = g if isinstance(T, int) else T * 2 + g
                pe.wait_ge(gelued, (group + 1) * FC)
                if not isinstance(T, int) or g >= 2:
                    pe.wait_ge(res_made, group - 1)
                for b in range(GROUP):
                    to = ybank[g % 2][:, b * D:(b + 1) * D]
                    for c in range(FC):
                        pe.matmul(to, hT[:, g % 2, c, b * P:(b + 1) * P], w2[:, c * D:(c + 1) * D],
                                  start=(c == 0), stop=False)
                    mm = pe.matmul(to, ones3[:, :], bparts[:, D:2 * D], start=False, stop=True)
                mm.then_inc(y_done, 1)

            up(0, 0)
            up(0, 1)
            down(0, 0)
            up(0, 2)
            down(0, 1)
            with pe.Fori(1, GROUPS // 2 - 1) as T:
                up(T, 1)
                down(T, 0)
                up(T, 2)
                down(T, 1)
            up(0, GROUPS - 1)
            down(0, GROUPS - 2)
            down(0, GROUPS - 1)


def kernel(**inputs):
    import numpy as np
    import concourse.bacc as bacc
    from concourse.bass_utils import run_bass_kernel_spmd

    a = {k: np.asarray(v) for k, v in inputs.items()}
    laid = {
        "x": a["x"],
        "ctxT": a["ctx_1024"].transpose(2, 0, 1),
        "g_xattn": a["g_xattn"], "g_ffn": a["g_ffn"],
        "Wq": a["L0_xattn_W_q"].transpose(1, 2, 0).reshape(D, D),
        "Wk": a["L0_xattn_W_k"].transpose(1, 2, 0).reshape(D, D),
        "Wv": a["L0_xattn_W_v"].transpose(1, 0, 2).reshape(D, D),
        "WoT": a["L0_xattn_W_o"].T,
        "b_o": a["L0_xattn_b_o"].reshape(1, D),
        "W1T": a["L0_ffn_W1"].T,
        "b1": a["L0_ffn_b1"].reshape(FC, P).T,
        "W2T": a["L0_ffn_W2"].T.reshape(FC, P, D).transpose(1, 0, 2),
        "b2": a["L0_ffn_b2"].reshape(1, D),
    }
    nc = bacc.Bacc("TRN2", target_bir_lowering=False, num_devices=1)
    arrays, aps = {}, []
    for name, v in laid.items():
        arrays[name] = np.ascontiguousarray(v)
        aps.append(nc.dram_tensor(name, arrays[name].shape, F32, kind="ExternalInput").ap())
    out = nc.dram_tensor("out", (B, P, D), F32, kind="ExternalOutput").ap()
    part_dram = nc.dram_tensor("part_dram", (3, 2, NPART, P, P), BF16, kind="Internal").ap()
    build(nc, *aps, out, part_dram)
    r = run_bass_kernel_spmd(nc, [arrays], core_ids=[0])
    return r.results[0]["out"]
```

```python
from contextlib import ExitStack

import concourse.bass as bass
from concourse import mybir

P = 128
D = 128
B = 32
H = 16
DK = D // H
FF = 4 * D
FC = FF // P
NPART = 3
PROD = NPART * NPART * DK
MROW = 96
QUAD = 4
UNITS = H // QUAD
PAIRS = H // 2
VW = 2 * DK + 1
VLAG = 3
PRING = 3
FILL = 6
BODY = 6
LEAD, LAG = 7, 5
RING = 6
FIRST = LAG
LOOPS = (B - LEAD - 1 - FIRST) // BODY
LAST = FIRST + LOOPS * BODY
GROUP = 4
GROUPS = B // GROUP
OVERLAP = B + 1
CTX = 2
XFIRST, XNEXT = 2, 8
LN_EPS = 1e-5
TWO_ONES = 1 + 0x3F80 / 2 ** 23

ALU = mybir.AluOpType
ACT = mybir.ActivationFunctionType
AX = mybir.AxisListType
F32 = mybir.dt.float32
BF16 = mybir.dt.bfloat16
assert BODY % RING == 0 and RING % CTX == 0 and B % CTX == 0


def entry(T, m):
    return m if isinstance(T, int) else T * BODY + m


def live(T, m):
    return not isinstance(T, int) or 0 <= m < B


def steps(T, m, per=1, part=None):
    part = per if part is None else part
    if isinstance(T, int):
        return 0 if m < 0 else per * m + part if m < B else per * B
    assert per * m + part > 0
    return T * (BODY * per) + (per * m + part)


def after(eng, sem, T, m, per=1, part=None):
    value = steps(T, m, per, part)
    if not isinstance(value, int) or value > 0:
        eng.wait_ge(sem, value)


def transfers(T, m, ring, per=1):
    if isinstance(T, int):
        return 0 if m < 0 else 16 * per * (m // ring + 1)
    assert m // ring + 1 > 0
    return T * (16 * per * (BODY // ring)) + 16 * per * (m // ring + 1)


def landed(eng, sems, T, m, per=1):
    value = transfers(T, m, len(sems), per)
    if not isinstance(value, int) or value > 0:
        eng.wait_ge(sems[m % len(sems)], value)


def periods(eng, period, last=B + LAG):
    for n in range(-LEAD - 1, FIRST):
        period(0, n)
    with eng.Fori(0, LOOPS) as T:
        for n in range(FIRST, FIRST + BODY):
            period(T, n)
    for n in range(LAST, last):
        period(0, n)


def build(nc, x, ctxT, W_attn, W_ffn, gates, biases, out, part_dram):
    with ExitStack() as es:
        def sb(name, shape, dt=F32):
            return es.enter_context(nc.sbuf_tensor(name, shape, dt))

        def ps(name, shape, dt=F32):
            return es.enter_context(nc.psum_tensor(name, shape, dt))

        def sem(name):
            return es.enter_context(nc.semaphore(name))

        xs = sb("xs", [P, B, D])
        ctx_sb = sb("ctx_sb", [D, RING, P])
        x2T = sb("x2T", [D, B * P])
        w_attn = sb("w_attn", [D, 4, D])
        wq, wk, wv, wo = (w_attn[:, i] for i in range(4))
        w_ffn = sb("w_ffn", [P, 2 * FF + FC])
        w1, w2, b1_sb = w_ffn[:, 0:FF], w_ffn[:, FF:2 * FF], w_ffn[:, 2 * FF:]
        tern = sb("tern", [P, 2, FF])
        wsum = sb("wsum", [P, 2])
        wscale = sb("wscale", [P, 3, 2])
        gate = sb("gate", [P, 2])
        tgate = sb("tgate", [P, 2])
        brow = sb("brow", [1, 2 * D])
        brest = sb("brest", [1, 2, 2 * D])
        bsplit = sb("bsplit", [1, NPART, 2 * D], BF16)
        bparts = sb("bparts", [NPART, 2 * D], BF16)
        ones3 = sb("ones3", [NPART, P], BF16)
        ones = sb("ones", [P, P])
        ident = sb("ident", [P, P])
        identb = sb("identb", [P, P], BF16)
        mhalf = sb("mhalf", [P, 2])

        st1 = sb("st1", [P, 2, 6])
        mv = sb("mv", [P, 2, 2, 2])
        ve = sb("ve", [P, 2, 2])
        negmean = sb("negmean", [P, 2])
        rstd = sb("rstd", [P, 2, 2])
        xh = sb("xh", [P, 2, D])
        xhT = sb("xhT", [D, 2, P])
        parts = sb("parts", [P, PRING, 2, NPART, P], BF16)
        rest = sb("rest", [P, 2, 2, P])
        qa = sb("qa", [P, RING, H, P], BF16)
        ka = sb("ka", [P, RING, H, P], BF16)
        va = sb("va", [P, RING, PAIRS, VW])
        nmax = sb("nmax", [P, 2, H])
        nrest = sb("nrest", [P, 2, 2, H])
        npart = sb("npart", [P, 2, P // H, H], BF16)
        zeros = sb("zeros", [P, 2 * P])
        pairs = sb("pairs", [P, 2 * P])
        nT = sb("nT", [NPART * H, 2, P], BF16)
        probs = sb("probs", [P, 2, UNITS, QUAD * P])
        oT = sb("oT", [P, 2, 4 * P])
        rden = sb("rden", [P, 2, H])
        on = sb("on", [P, 2, D])
        onT = sb("onT", [D, 2, P])
        x2 = sb("x2", [P, 2, D])
        st2 = sb("st2", [P, 2, 6])
        xh2 = sb("xh2", [P, 2, D])
        hT = sb("hT", [P, 2, FC, GROUP * P])
        res = sb("res", [P, 2, GROUP, D])

        pS = [ps(f"pS{i}", [P, QUAD * P]) for i in range(2)]
        pT = [ps(f"pT{i}", [P, QUAD * P]) for i in range(2)]
        pO = ps("pO", [P, 4 * P])
        pR = ps("pR", [P, 4 * P])
        pA = ps("pA", [P, 4 * P])
        pB = ps("pB", [P, 4 * P])
        pAb = pA[:, P:2 * P].bitcast(BF16)

        def proj_bank(T, m):
            return pB if isinstance(T, int) and m < FILL and m % 2 else pA

        hbank = [pS[0], pS[1], pT[0], pT[1]]
        ybank = [pA, pO]

        x_in = [sem(f"x_in{i}") for i in range(3)]
        ctx_in = [sem(f"ctx_in{i}") for i in range(RING // CTX)]
        proj_in, w_in, small_in, bias_in = sem("proj_in"), sem("w_in"), sem("small_in"), sem("bias_in")
        parts_stored = [sem(f"parts_stored{i}") for i in range(RING)]
        aug_loaded = [sem(f"aug_loaded{i}") for i in range(RING)]
        max_loaded = [sem(f"max_loaded{i}") for i in range(2)]
        out_stored = [sem(f"out_stored{i}") for i in range(2)]
        ident_zero, ident_made, identb_made, consts_made = (
            sem("ident_zero"), sem("ident_made"), sem("identb_made"), sem("consts_made"))
        pool_pad, dve_pad, act_pad, pairs_made = sem("pool_pad"), sem("dve_pad"), sem("act_pad"), sem("pairs_made")
        va_made, pO_made = sem("va_made"), sem("pO_made")
        gates_made, bias_step, bias_split = sem("gates_made"), sem("bias_step"), sem("bias_split")
        wsum_made, wtotal_made, wstep, w_made = sem("wsum_made"), sem("wtotal_made"), sem("wstep"), sem("w_made")
        scored, keyed, pv_done = sem("scored"), sem("keyed"), sem("pv_done")
        o_turned, on_turned, wo_done = sem("o_turned"), sem("on_turned"), sem("wo_done")
        max_turned, xh_turned, projected, v_projected, xh2_turned = sem("max_turned"), sem("xh_turned"), sem("projected"), sem("v_projected"), sem("xh2_turned")
        reduced, bn1_done, mv1_done = sem("reduced"), sem("bn1_done"), sem("mv1_done")
        xh_made, rest_made, rden_made, on_made = sem("xh_made"), sem("rest_made"), sem("rden_made"), sem("on_made")
        x2_made, bn2_done, mv2_done, stats_made = sem("x2_made"), sem("bn2_done"), sem("mv2_done"), sem("stats_made")
        exped, max_copied, o_copied, on_copied = sem("exped"), sem("max_copied"), sem("o_copied"), sem("on_copied")
        xh_copied, v_copied, first_made, x2_kept, xh2_copied = (
            sem("xh_copied"), sem("v_copied"), sem("first_made"), sem("x2_kept"), sem("xh2_copied"))
        nsplit, rstd_made, mid_made, parts_made, xh2_made = (
            sem("nsplit"), sem("rstd_made"), sem("mid_made"), sem("parts_made"), sem("xh2_made"))
        hidden, gelued, y_done, res_made = sem("hidden"), sem("gelued"), sem("y_done"), sem("res_made")

        def qpad_sem(m):
            return (pool_pad, m + 1) if m < RING - 1 else (act_pad, 2)

        def kpad_sem(m):
            return (dve_pad, m + 1) if m < 3 else (act_pad, (1, 3, 4)[m - 3])

        x_dram = x.rearrange("b s d -> s b d")
        out_dram = out.rearrange("(g b) s d -> g s b d", b=GROUP)
        block = es.enter_context(nc.Block())

        @block.sync
        def _(sp):
            def load_context(T, m):
                after(sp, v_projected, T, m - RING + CTX - 1)
                sp.dma_start(ctx_sb[:, m % RING:m % RING + CTX], ctxT[:, bass.ds(entry(T, m), CTX), :]
                             ).then_inc(ctx_in[m % RING // CTX], 16)

            edges = [0, XFIRST, XNEXT, B]
            for i in range(3):
                part = slice(edges[i], edges[i + 1])
                sp.dma_start(xs[:, part, :], x_dram[:, part, :]).then_inc(x_in[i], 16)
                load_context(0, i * CTX)

            def period(T, n):
                m = n + 1
                if live(T, m):
                    after(sp, max_copied, T, m)
                    sp.dma_start(qa[MROW:MROW + NPART, m % RING], nT[:, m % 2]).then_inc(max_loaded[m % 2], 16)
                m = n + LEAD - 1
                if live(T, m):
                    after(sp, parts_made, T, m)
                    sp.dma_start(part_dram[m % RING].rearrange("w i r s -> r (w i) s"),
                                 parts[:, m % PRING].rearrange("p w i s -> p (w i) s")
                                 ).then_inc(parts_stored[m % RING], 16)
                m = n + LEAD - 2
                if live(T, m):
                    if isinstance(T, int) and m < RING:
                        sp.wait_ge(qpad_sem(m)[0], qpad_sem(m)[1])
                        sp.wait_ge(kpad_sem(m)[0], kpad_sem(m)[1])
                    landed(sp, parts_stored, T, m)
                    qsrc = part_dram[m % RING, 0].rearrange("i (k h) s -> (i k) (h s)", k=DK)
                    ksrc = part_dram[m % RING, 1].rearrange("j (k h) s -> k j (h s)", k=DK)
                    sp.dma_start(qa[0:PROD, m % RING], qsrc.unsqueeze(1).to_broadcast([NPART * DK, NPART, H * P])
                                 ).then_inc(aug_loaded[m % RING], 16)
                    for i in range(NPART):
                        rows = slice(i * NPART * DK, (i + 1) * NPART * DK)
                        sp.dma_start(ka[rows, m % RING], ksrc).then_inc(aug_loaded[m % RING], 16)
                m = n + LEAD - VLAG + RING - CTX + 1
                if live(T, m) and m % CTX == 0 and m >= RING:
                    load_context(T, m)
                if isinstance(T, int) and n == -3:
                    sp.wait_ge(bias_split, 1)
                    sp.dma_start(bparts[:, :], bsplit[:, :, :]).then_inc(bias_in, 16)

            periods(sp, period)

            def store(T, g):
                group = g if isinstance(T, int) else T * 2 + g
                sp.wait_ge(res_made, group + 1)
                sp.dma_start(out_dram[group], res[:, g % 2]).then_inc(out_stored[g % 2], 16)

            with sp.Fori(0, GROUPS // 2) as T:
                for g in range(2):
                    store(T, g)
            for g in range(2):
                sp.wait_ge(out_stored[g], 16 * (GROUPS // 2))

        @block.gpsimd
        def _(pool):
            pool.memset(ident[:, :], 0.0).then_inc(ident_zero, 1)
            pool.wait_ge(ident_zero, 1)
            pool.affine_select(out=ident[:, :], in_=ident[:, :], compare_op=ALU.not_equal, fill=1.0, base=0,
                               pattern=[[-1, P]], channel_multiplier=1).then_inc(ident_made, 1)
            pool.memset(zeros[:, :], 0.0).then_inc(consts_made, 1)
            pool.memset(npart[:, :, :, :], 0.0).then_inc(consts_made, 1)
            pool.memset(mhalf[:, :], -0.5).then_inc(consts_made, 1)
            pool.wait_ge(consts_made, 3)
            def period(T, n):
                m, k, s = n + LEAD, n - 4, n % 2
                which = slice(0 if live(T, k) else 1, 2 if live(T, m) else 1)
                if live(T, m) or live(T, k):
                    pool.wait_ge(stats_made, T * BODY + (n + LEAD + 1))
                    if live(T, m):
                        after(pool, xh_made, T, m - 2)
                    pool.tensor_tensor(rstd[:, s, which], ve[:, 1 - s, which], mhalf[:, which], ALU.pow
                                       ).then_inc(rstd_made, 1)
                if isinstance(T, int):
                    for m in {-LEAD - 1: (0, 1), -LEAD: (2,), 1 - LEAD: (3, 4)}.get(n, ()):
                        if n > -LEAD - 1:
                            pool.wait_ge(rstd_made, n + LEAD + 1)
                        pool.memset(qa[64:P, m].rearrange("p h s -> p (h s)").bitcast(F32), 0.0).then_inc(pool_pad, 1)
                        pool.wait_ge(pool_pad, m + 1)
                m = n + 1
                if live(T, m):
                    s = m % 2
                    after(pool, reduced, T, m, UNITS)
                    after(pool, max_turned, T, m - 2)
                    pool.tensor_tensor(npart[:, s, 0], nmax[:, s], zeros[:, 0:H], ALU.add).then_inc(nsplit, 1)
                    after(pool, nsplit, T, m, 4, 1)
                    pool.tensor_tensor(nrest[:, s, 0], nmax[:, s], npart[:, s, 0], ALU.subtract).then_inc(nsplit, 1)
                    after(pool, nsplit, T, m, 4, 2)
                    pool.tensor_tensor(npart[:, s, 1], nrest[:, s, 0], zeros[:, 0:H], ALU.add).then_inc(nsplit, 1)
                    after(pool, nsplit, T, m, 4, 3)
                    pool.tensor_tensor(npart[:, s, 2], nrest[:, s, 0], npart[:, s, 1], ALU.subtract
                                       ).then_inc(nsplit, 1)
                if live(T, k):
                    pool.wait_ge(rstd_made, T * BODY + (n + LEAD + 1))
                m = n + LEAD - 1
                s = m % 2
                if live(T, m):
                    after(pool, rest_made, T, m)
                    landed(pool, parts_stored, T, m - PRING)
                    pool.tensor_tensor(parts[:, m % PRING, :, 1], rest[:, s], zeros[:, :].rearrange("p (w s) -> p w s", w=2),
                                       ALU.add).then_inc(mid_made, 1)
                if live(T, k):
                    if isinstance(T, int):
                        after(pool, xh2_turned, T, k - 2)
                    pool.tensor_scalar(xh2[:, k % 2], x2[:, k % 2], negmean[:, 1 - n % 2:2 - n % 2],
                                       rstd[:, n % 2, 0:1], ALU.add, ALU.mult).then_inc(xh2_made, 1)
                if live(T, m):
                    after(pool, mid_made, T, m)
                    pool.tensor_tensor(parts[:, m % PRING, :, 2], rest[:, s], parts[:, m % PRING, :, 1], ALU.subtract
                                       ).then_inc(parts_made, 1)

            periods(pool, period)

        @block.scalar
        def _(act):
            act.dma_start(w_attn[:, :, :], W_attn).then_inc(proj_in, 16)
            act.dma_start(gate[:, :], gates.partition_broadcast(P)).then_inc(small_in, 16)
            act.dma_start(brow[:, :], biases).then_inc(small_in, 16)
            act.dma_start(w_ffn[:, :], W_ffn).then_inc(w_in, 16)
            act.wait_ge(small_in, 16 * 2)
            act.activation(tgate[:, :], gate[:, :], ACT.Tanh).then_inc(gates_made, 1)
            act.wait_ge(va_made, 1)

            def pad(rows, slot, value):
                dst = rows[64:P, slot].rearrange("p h s -> p (h s)").bitcast(F32).rearrange("p (a c) -> p a c", c=2 * P)
                act.copy(dst, value[64:P].unsqueeze(1).to_broadcast([P - 64, H * P // (4 * P), 2 * P])
                         ).then_inc(act_pad, 1)

            def exp(T, n, u):
                if not live(T, n):
                    return
                after(act, keyed, T, n, UNITS, u + 1)
                after(act, pv_done, T, n - 2, 2, u // 2 + 1)
                act.activation(probs[:, n % 2, u], pT[u % 2][:, :], ACT.Exp, scale=float(DK) ** -0.5
                               ).then_inc(exped, 1)

            def period(T, n):
                exp(T, n - 1, 2)
                exp(T, n - 1, 3)
                m = n + LEAD
                if live(T, m):
                    if live(T, n + 1):
                        after(act, max_turned, T, n + 1)
                    else:
                        after(act, xh_turned, T, m)
                    act.copy(xhT[:, m % 2], proj_bank(T, m)[:, 0:P]).then_inc(xh_copied, 1)
                m = n + 1
                if live(T, m):
                    s = m % 2
                    after(act, max_turned, T, m)
                    landed(act, max_loaded, T, m - 2)
                    act.copy(nT[:, s], pAb[0:NPART * H, 0:P]).then_inc(max_copied, 1)
                if isinstance(T, int) and n == -LEAD:
                    act.wait_ge(pairs_made, 1)
                    pad(ka, 3, pairs)
                if isinstance(T, int) and n == -3:
                    act.wait_ge(consts_made, 3)
                    pad(qa, 5, zeros)
                if isinstance(T, int) and n in (-2, -1):
                    pad(ka, n + 6, pairs)
                m = n - 3
                if live(T, m):
                    after(act, x2_made, T, m)
                    act.copy(xs[:, entry(T, m), :], x2[:, m % 2]).then_inc(x2_kept, 1)
                m = n - 5
                if live(T, m):
                    after(act, xh2_turned, T, m)
                    e = entry(T, m)
                    act.copy(x2T[:, bass.ds(e * P, P)], pB[:, 0:P]).then_inc(xh2_copied, 1)
                exp(T, n, 0)
                m = n + LEAD
                if live(T, m - VLAG):
                    after(act, v_projected, T, m - VLAG)
                if live(T, m):
                    if m < VLAG:
                        after(act, projected, T, m)
                    stored_before(act, T, m)
                    act.copy(parts[:, m % PRING, :, 0], proj_bank(T, m)[:, 0:2 * P].rearrange("p (w s) -> p w s", w=2)
                             ).then_inc(first_made, 1)
                m = n + LEAD - VLAG
                if live(T, m):
                    after(act, pv_done, T, m - RING, 2)
                    act.copy(va[:, m % RING, :, 0:2 * DK],
                             proj_bank(T, n + LEAD)[:, 2 * P:3 * P].rearrange("p (j w) -> p j w", j=PAIRS)).then_inc(v_copied, 1)
                m = n - 2
                if live(T, m):
                    after(act, on_turned, T, m)
                    act.copy(onT[:, m % 2], pB[:, 0:P]).then_inc(on_copied, 1)
                exp(T, n, 1)
                m = n - 1
                if live(T, m):
                    after(act, pv_done, T, m, 2)
                    after(act, o_turned, T, m - 2)
                    act.copy(oT[:, m % 2], pO[:, :]).then_inc(o_copied, 1)

            def stored_before(eng, T, m):
                landed(eng, parts_stored, T, m - PRING)

            periods(act, period, OVERLAP)

            def gelu(T, g):
                group = g if isinstance(T, int) else T * 2 + g
                for c in range(FC):
                    act.wait_ge(hidden, group * FC + (c + 1))
                    if not isinstance(T, int) or g >= 2:
                        act.wait_ge(y_done, group - 1)
                    act.activation(hT[:, g % 2, c], hbank[c][:, :], ACT.Gelu, bias=b1_sb[:, c:c + 1]
                                   ).then_inc(gelued, 1)

            gelu(0, 0)
            period(0, OVERLAP)
            gelu(0, 1)
            period(0, OVERLAP + 1)
            gelu(0, 2)
            period(0, OVERLAP + 2)
            period(0, OVERLAP + 3)
            with act.Fori(1, GROUPS // 2 - 1) as T:
                gelu(T, 1)
                gelu(T, 2)
            gelu(0, GROUPS - 1)

        @block.vector
        def _(dve):
            dve.memset(ones3[:, :], 1.0).then_inc(identb_made, 1)
            dve.memset(va[:, :, :, :], 1.0).then_inc(va_made, 1)
            dve.memset(pairs[:, :], TWO_ONES).then_inc(pairs_made, 1)
            dve.wait_ge(ident_made, 1)
            dve.tensor_copy(identb[:, :], ident[:, :]).then_inc(identb_made, 1)

            def split_biases():
                dve.wait_ge(small_in, 16 * 2)
                dve.tensor_copy(bsplit[:, 0], brow[:, :]).then_inc(bias_step, 1)
                dve.wait_ge(bias_step, 1)
                dve.tensor_tensor(brest[:, 0], brow[:, :], bsplit[:, 0], ALU.subtract).then_inc(bias_step, 1)
                dve.wait_ge(bias_step, 2)
                dve.tensor_copy(bsplit[:, 1], brest[:, 0]).then_inc(bias_step, 1)
                dve.wait_ge(bias_step, 3)
                dve.tensor_tensor(bsplit[:, 2], brest[:, 0], bsplit[:, 1], ALU.subtract).then_inc(bias_split, 1)

            def weight_sums():
                dve.wait_ge(w_in, 16)
                dve.memset(ones[:, :], 1.0)
                for i, w in enumerate((w1, w2)):
                    ins = dve.tensor_reduce(wsum[:, i:i + 1], w[:, :], AX.X, ALU.add, apply_absolute_value=True)
                ins.then_inc(wsum_made, 1)

            def thresholds():
                dve.wait_ge(wtotal_made, 1)
                dve.tensor_scalar(wscale[:, 0], pS[0][:, 0:2], 1.0 / (D * FF), 1e-8, ALU.mult, ALU.max).then_inc(wstep, 1)
                dve.wait_ge(wstep, 1)
                dve.tensor_scalar(wscale[:, 1], wscale[:, 0], 0.5, None, ALU.mult).then_inc(wstep, 1)
                dve.tensor_scalar(wscale[:, 2], wscale[:, 0], -0.5, None, ALU.mult).then_inc(wstep, 1)

            def ternary(i, half):
                w, step = (w1, w2)[i], 3 + 3 * i
                if half == 0:
                    dve.wait_ge(wstep, step)
                    dve.tensor_scalar(tern[:, 0], w[:, :], wscale[:, 1, i:i + 1], None, ALU.is_gt).then_inc(wstep, 1)
                    dve.wait_ge(wstep, step + 1)
                    dve.scalar_tensor_tensor(out=tern[:, 1], in0=w[:, :], scalar=wscale[:, 2, i:i + 1],
                                             in1=tern[:, 0], op0=ALU.is_lt, op1=ALU.subtract).then_inc(wstep, 1)
                else:
                    dve.wait_ge(wstep, step + 2)
                    dve.tensor_tensor(tern[:, 0], w[:, :], tern[:, 1], ALU.add).then_inc(wstep, 1)
                    dve.wait_ge(wstep, step + 3)
                    dve.tensor_tensor(w[:, :], w[:, :], tern[:, 0], ALU.subtract).then_inc(w_made, 1)
                    dve.wait_ge(w_made, i + 1)

            def row_max(T, m, u):
                if not live(T, m):
                    return
                after(dve, scored, T, m, UNITS, u + 1)
                if u == 0:
                    after(dve, nsplit, T, m - 2, 4)
                dve.tensor_reduce(nmax[:, m % 2, u * QUAD:(u + 1) * QUAD],
                                  pS[u % 2][:, :].rearrange("p (h s) -> p h s", h=QUAD), AX.X, ALU.max,
                                  negate=True).then_inc(reduced, 1)

            def statistics(T, n):
                k, m = n - 3, n + LEAD + 1
                which = slice(0 if live(T, k) else 1, 2 if live(T, m) else 1)
                s = n % 2
                if live(T, k):
                    dve.bn_aggr(mv[:, s, 0], st2[:, k % 2]).then_inc(mv2_done, 1)
                if live(T, m):
                    dve.bn_aggr(mv[:, s, 1], st1[:, m % 2]).then_inc(mv1_done, 1)
                if live(T, k):
                    after(dve, mv2_done, T, k)
                    dve.tensor_scalar(negmean[:, s:s + 1], mv[:, s, 0, 0:1], -1.0, None, ALU.mult)
                if live(T, m):
                    after(dve, mv1_done, T, m)
                if live(T, k) or live(T, m):
                    dve.tensor_scalar(ve[:, s, which], mv[:, s, which, 1], LN_EPS, None, ALU.add).then_inc(stats_made, 1)

            def first_norm(T, n):
                m = n + LEAD
                if live(T, m):
                    dve.wait_ge(rstd_made, T * BODY + (n + LEAD + 1))
                    after(dve, xh_turned, T, m - 2)
                    dve.tensor_scalar(xh[:, m % 2], xs[:, entry(T, m), :], mv[:, (n - 1) % 2, 1, 0:1],
                                      rstd[:, n % 2, 1:2], ALU.subtract, ALU.mult).then_inc(xh_made, 1)

            def period(T, n):
                row_max(T, n + 2, 0)
                if not (isinstance(T, int) and n + LEAD < FILL):
                    first_norm(T, n)
                row_max(T, n + 2, 1)
                k = n - 3
                if live(T, k):
                    if isinstance(T, int) and k == 0:
                        dve.wait_ge(gates_made, 1)
                    after(dve, wo_done, T, k)
                    after(dve, xh2_made, T, k - 2)
                    after(dve, x2_kept, T, k - 2)
                    dve.scalar_tensor_tensor(out=x2[:, k % 2], in0=pB[:, 0:P], scalar=tgate[:, 0:1],
                                             in1=xs[:, entry(T, k), :], op0=ALU.mult, op1=ALU.add).then_inc(x2_made, 1)
                m = n + LEAD + 1
                if live(T, m):
                    if isinstance(T, int) and m in (0, XFIRST, XNEXT):
                        dve.wait_ge(x_in[(0, XFIRST, XNEXT).index(m)], 16)
                    dve.bn_stats(st1[:, m % 2], xs[:, entry(T, m), :]).then_inc(bn1_done, 1)
                row_max(T, n + 2, 2)
                m = n - 2
                if live(T, m):
                    after(dve, o_turned, T, m)
                    den = pR[:, :].rearrange("p (b c) -> p b c", b=2)[:, :, 2 * DK:2 * P]
                    den = den.rearrange("p b (r c) -> p b r c", r=2)[:, :, :, 0:97:32]
                    dve.reciprocal(rden[:, m % 2].rearrange("p (b r j) -> p b r j", b=2, r=2), den
                                   ).then_inc(rden_made, 1)
                if live(T, k):
                    after(dve, x2_made, T, k)
                    dve.bn_stats(st2[:, k % 2], x2[:, k % 2]).then_inc(bn2_done, 1)
                if live(T, m):
                    after(dve, rden_made, T, m)
                    dve.tensor_tensor(on[:, m % 2].rearrange("p (h k) -> p h k", h=H),
                                      pR[:, :].rearrange("p (h c) -> p h c", h=H)[:, :, 0:DK],
                                      rden[:, m % 2].unsqueeze(2).to_broadcast([P, H, DK]), ALU.mult
                                      ).then_inc(on_made, 1)
                if live(T, k):
                    after(dve, bn2_done, T, k)
                if live(T, n + LEAD + 1):
                    after(dve, bn1_done, T, n + LEAD + 1)
                row_max(T, n + 2, 3)
                statistics(T, n)
                if isinstance(T, int):
                    for m in {-LEAD - 1: (0,), -LEAD: (1, 2)}.get(n, ()):
                        dve.memset(ka[64:P, m].rearrange("p h s -> p (h s)").bitcast(F32), TWO_ONES).then_inc(dve_pad, 1)
                if isinstance(T, int) and n == 1 - LEAD:
                    split_biases()
                if isinstance(T, int) and n == 2 - LEAD:
                    dve.memset(pO[:, :], 0.0).then_inc(pO_made, 1)
                if isinstance(T, int) and n + LEAD + 1 < FILL:
                    first_norm(T, n + 1)
                m = n + LEAD
                if live(T, m):
                    s = m % 2
                    after(dve, first_made, T, m)
                    after(dve, v_copied, T, m - VLAG)
                    after(dve, parts_made, T, m - 2)
                    dve.tensor_tensor(rest[:, s], proj_bank(T, m)[:, 0:2 * P].rearrange("p (w s) -> p w s", w=2),
                                      parts[:, m % PRING, :, 0], ALU.subtract).then_inc(rest_made, 1)
                if isinstance(T, int) and n == B - 2:
                    weight_sums()
                if isinstance(T, int) and n == B - 1:
                    thresholds()
                    ternary(0, 0)
                    ternary(0, 1)
                if isinstance(T, int) and n == B:
                    ternary(1, 0)
                    ternary(1, 1)

            periods(dve, period, OVERLAP)

            def residual(T, g):
                group = g if isinstance(T, int) else T * 2 + g
                dve.wait_ge(y_done, group + 1)
                if not isinstance(T, int):
                    dve.wait_ge(out_stored[g], T * 16)
                dve.scalar_tensor_tensor(out=res[:, g], in0=ybank[g][:, :].rearrange("p (b d) -> p b d", b=GROUP),
                                         scalar=tgate[:, 1:2], in1=xs[:, bass.ds(group * GROUP, GROUP), :],
                                         op0=ALU.mult, op1=ALU.add).then_inc(res_made, 1)

            period(0, OVERLAP)
            dve.wait_ge(x2_kept, 2 * GROUP)
            residual(0, 0)
            period(0, OVERLAP + 1)
            residual(0, 1)
            dve.wait_ge(x2_kept, B)
            with dve.Fori(1, GROUPS // 2) as T:
                for g in range(2):
                    residual(T, g)

        @block.tensor
        def _(pe):
            pe.wait_ge(ident_made, 1)
            pe.wait_ge(identb_made, 2)
            pe.wait_ge(proj_in, 16)

            def scores(T, n, u):
                if not live(T, n):
                    return
                if u == 0:
                    landed(pe, aug_loaded, T, n, 1 + NPART)
                after(pe, reduced, T, n if u >= 2 else n - 1, UNITS, (u - 2) % UNITS + 1)
                for j in range(QUAD):
                    h = u * QUAD + j
                    mm = pe.matmul(pS[u % 2][:, j * P:(j + 1) * P], qa[0:MROW, n % RING, h], ka[0:MROW, n % RING, h],
                                   start=True, stop=True)
                mm.then_inc(scored, 1)

            def keyed_scores(T, n, u):
                if not live(T, n):
                    return
                if u == 0:
                    landed(pe, max_loaded, T, n)
                after(pe, exped, T, n if u >= 2 else n - 1, UNITS, (u - 2) % UNITS + 1)
                for j in range(QUAD):
                    h = u * QUAD + j
                    mm = pe.matmul(pT[u % 2][:, j * P:(j + 1) * P], ka[:, n % RING, h], qa[:, n % RING, h],
                                   start=True, stop=True)
                mm.then_inc(keyed, 1)

            def probs_v(T, n, b):
                if not live(T, n):
                    return
                after(pe, exped, T, n, UNITS, 2 * b + 2)
                if b == 0:
                    if isinstance(T, int) and n == 0:
                        pe.wait_ge(pO_made, 1)
                    after(pe, v_copied, T, n)
                    after(pe, o_copied, T, n - 1)
                for j in range(4):
                    pr = probs[:, n % 2, 2 * b:2 * b + 2, j * P:(j + 1) * P]
                    mm = pe.matmul(pO[32 * j:32 * j + VW, b * 2 * P:(b + 1) * 2 * P].rearrange("p (r s) -> p r s", r=2),
                                   va[:, n % RING, 4 * b + j], pr, start=True, stop=True)
                mm.then_inc(pv_done, 1)

            def turn_o(T, n):
                if not live(T, n):
                    return
                after(pe, o_copied, T, n)
                after(pe, on_made, T, n - 1)
                for b in range(2):
                    for r in range(2):
                        at = b * 2 * P + r * (P - DK)
                        mm = pe.transpose(pR[:, at:at + P], oT[:, n % 2, (2 * b + r) * P:(2 * b + r + 1) * P], ident[:, :])
                mm.then_inc(o_turned, 1)

            def turn_on(T, n):
                if not live(T, n):
                    return
                after(pe, on_made, T, n)
                after(pe, xh2_copied, T, n - 3)
                pe.transpose(pB[:, 0:P], on[:, n % 2], ident[:, :]).then_inc(on_turned, 1)

            def project_out(T, n):
                if not live(T, n):
                    return
                after(pe, on_copied, T, n)
                if isinstance(T, int) and n == 0:
                    pe.wait_ge(bias_in, 16)
                pe.matmul(pB[:, 0:P], onT[:, n % 2], wo[:, :], start=True, stop=False)
                pe.matmul(pB[:, 0:P], ones3[:, :], bparts[:, 0:D], start=False, stop=True).then_inc(wo_done, 1)

            def turn_xh2(T, n):
                if not live(T, n):
                    return
                after(pe, xh2_made, T, n)
                after(pe, x2_made, T, n + 2)
                if isinstance(T, int):
                    after(pe, xh2_copied, T, n - 1)
                pe.transpose(pB[:, 0:P], xh2[:, n % 2], ident[:, :]).then_inc(xh2_turned, 1)

            def turn_max(T, n):
                if not live(T, n):
                    return
                after(pe, nsplit, T, n, 4)
                if not live(T, n + LEAD - 1):
                    after(pe, v_copied, T, n - 2 + LEAD - VLAG)
                    after(pe, rest_made, T, n - 2 + LEAD)
                pe.transpose(pAb[:, 0:P], npart[:, n % 2].rearrange("p i h -> p (i h)"), identb[:, :]
                             ).then_inc(max_turned, 1)

            def turn_xh(T, n):
                if not live(T, n):
                    return
                after(pe, xh_made, T, n)
                last = n - 2 if isinstance(T, int) and n <= FILL else n - 1
                after(pe, rest_made, T, last)
                after(pe, v_copied, T, last - VLAG)
                pe.transpose(proj_bank(T, n)[:, 0:P], xh[:, n % 2], ident[:, :]).then_inc(xh_turned, 1)

            def project(T, n):
                bank = proj_bank(T, n)
                if live(T, n):
                    after(pe, xh_copied, T, n)
                    after(pe, max_copied, T, n - LEAD + 1)
                    if n % CTX == 0:
                        pe.wait_ge(ctx_in[n % RING // CTX], T * 16 * (BODY // RING) + 16 * (n // RING + 1))
                    pe.matmul(bank[:, 0:P], wq[:, :], xhT[:, n % 2], start=True, stop=True)
                    pe.matmul(bank[:, P:2 * P], wk[:, :], ctx_sb[:, n % RING], start=True, stop=True
                              ).then_inc(projected, 1)
                v = n - VLAG
                if live(T, v):
                    if not live(T, n):
                        after(pe, max_copied, T, n - LEAD + 1)
                        after(pe, v_copied, T, v - 1)
                    pe.matmul(bank[:, 2 * P:3 * P], ctx_sb[:, v % RING], wv[:, :], start=True, stop=True
                              ).then_inc(v_projected, 1)

            def period(T, n):
                scores(T, n + 2, 0)
                keyed_scores(T, n - 1, 2)
                scores(T, n + 2, 1)
                if isinstance(T, int) and n == B - 1:
                    pe.wait_ge(wsum_made, 1)
                    pe.wait_ge(reduced, B * UNITS)
                    pe.matmul(pS[0][:, 0:2], ones[:, :], wsum[:, :], start=True, stop=True).then_inc(wtotal_made, 1)
                project_out(T, n - 3)
                keyed_scores(T, n - 1, 3)
                probs_v(T, n - 1, 0)
                turn_o(T, n - 2)
                turn_xh(T, n + LEAD)
                turn_max(T, n + 1)
                scores(T, n + 2, 2)
                turn_xh2(T, n - 5)
                keyed_scores(T, n, 0)
                scores(T, n + 2, 3)
                project(T, n + LEAD)
                keyed_scores(T, n, 1)
                turn_on(T, n - 2)
                probs_v(T, n - 1, 1)
            periods(pe, period, OVERLAP)

            def up(T, g):
                group = g if isinstance(T, int) else T * 2 + g
                if isinstance(T, int) and g == 0:
                    pe.wait_ge(w_made, 1)
                    pe.wait_ge(reduced, B * UNITS)
                    pe.wait_ge(exped, B * UNITS)
                    pe.wait_ge(xh2_copied, 3 * GROUP)
                for c in range(FC):
                    if not isinstance(T, int) or g >= 1:
                        pe.wait_ge(gelued, (group - 1) * FC + (c + 1))
                    pe.matmul(hbank[c][:, :], w1[:, c * P:(c + 1) * P], x2T[:, bass.ds(group * GROUP * P, GROUP * P)],
                              start=True, stop=True).then_inc(hidden, 1)

            def down(T, g):
                group = g if isinstance(T, int) else T * 2 + g
                pe.wait_ge(gelued, (group + 1) * FC)
                if not isinstance(T, int) or g >= 2:
                    pe.wait_ge(res_made, group - 1)
                elif g == 0:
                    pe.wait_ge(w_made, 2)
                    pe.wait_ge(max_copied, B)
                    pe.wait_ge(v_copied, B)
                    pe.wait_ge(rest_made, B)
                else:
                    pe.wait_ge(o_copied, B)
                for b in range(GROUP):
                    to = ybank[g % 2][:, b * D:(b + 1) * D]
                    for c in range(FC):
                        pe.matmul(to, hT[:, g % 2, c, b * P:(b + 1) * P], w2[:, c * D:(c + 1) * D],
                                  start=(c == 0), stop=False)
                    mm = pe.matmul(to, ones3[:, :], bparts[:, D:2 * D], start=False, stop=True)
                mm.then_inc(y_done, 1)

            up(0, 0)
            project_out(0, B - 2)
            turn_o(0, B - 1)
            up(0, 1)
            turn_xh2(0, B - 4)
            turn_on(0, B - 1)
            down(0, 0)
            project_out(0, B - 1)
            turn_xh2(0, B - 3)
            up(0, 2)
            turn_xh2(0, B - 2)
            down(0, 1)
            turn_xh2(0, B - 1)
            pe.wait_ge(xh2_copied, B)
            with pe.Fori(1, GROUPS // 2 - 1) as T:
                up(T, 1)
                down(T, 0)
                up(T, 2)
                down(T, 1)
            up(0, GROUPS - 1)
            down(0, GROUPS - 2)
            down(0, GROUPS - 1)


def kernel(**inputs):
    import numpy as np
    import concourse.bacc as bacc
    from concourse.bass_utils import run_bass_kernel_spmd

    a = {k: np.asarray(v) for k, v in inputs.items()}
    W_attn = [a["L0_xattn_W_" + w].transpose(1, 2, 0).reshape(D, D) for w in "qk"]
    W_attn.append(a["L0_xattn_W_v"].reshape(2, 2, 4, D, DK).transpose(3, 0, 2, 1, 4).reshape(D, D))
    W_attn.append(a["L0_xattn_W_o"].T)
    laid = {
        "x": a["x"],
        "ctxT": a["ctx_1024"].transpose(2, 0, 1),
        "W_attn": np.stack(W_attn, 1),
        "W_ffn": np.concatenate([
            a["L0_ffn_W1"].T,
            a["L0_ffn_W2"].T.reshape(FC, P, D).transpose(1, 0, 2).reshape(P, FF),
            a["L0_ffn_b1"].reshape(FC, P).T], 1),
        "gates": np.concatenate([a["g_xattn"], a["g_ffn"]]),
        "biases": np.concatenate([a["L0_xattn_b_o"], a["L0_ffn_b2"]]).reshape(1, 2 * D),
    }
    nc = bacc.Bacc("TRN2", target_bir_lowering=False, num_devices=1)
    arrays, aps = {}, []
    for name, v in laid.items():
        arrays[name] = np.ascontiguousarray(v)
        aps.append(nc.dram_tensor(name, arrays[name].shape, F32, kind="ExternalInput").ap())
    out = nc.dram_tensor("out", (B, P, D), F32, kind="ExternalOutput").ap()
    part_dram = nc.dram_tensor("part_dram", (RING, 2, NPART, P, P), BF16, kind="Internal").ap()
    build(nc, *aps, out, part_dram)
    r = run_bass_kernel_spmd(nc, [arrays], core_ids=[0])
    return r.results[0]["out"]
```

```python
from contextlib import ExitStack

import concourse.bass as bass
from concourse import mybir

P = 128
D = 128
B = 32
H = 16
DK = D // H
FF = 4 * D
FC = FF // P
NPART = 3
PROD = NPART * NPART * DK
MROW = 96
QUAD = 4
UNITS = H // QUAD
PAIRS = H // 2
VW = 2 * DK + 1
VLAG = 3
PRING = 3
FILL = 6
BODY = 6
LEAD, LAG = 7, 5
RING = 6
FIRST = LAG
LOOPS = (B - LEAD - 1 - FIRST) // BODY
LAST = FIRST + LOOPS * BODY
GROUP = 4
GROUPS = B // GROUP
OVERLAP = B + 1
DPARTS = 3
WARM_TURN = {-1: 5, 0: 3}
WARM_BEFORE = {-7: 1, -6: 1, -5: 1, -4: 1, -3: 1, -1: 1}
WARM_AFTER = {-8: 7, -7: 3, -6: 3, -5: 3, -4: 3, -3: 2, -1: 1}
HALVES = range(GROUP // 2), range(GROUP // 2, GROUP)
CTX = 2
XEDGES = (0, 2, 8, 26, B)
XLATE = 2
TERNARY = {B - LEAD: (0, 0), B - 3: (0, 1), B - 1: (1, 0), B: (1, 1)}
LN_EPS = 1e-5
TWO_ONES = 1 + 0x3F80 / 2 ** 23

ALU = mybir.AluOpType
ACT = mybir.ActivationFunctionType
AX = mybir.AxisListType
F32 = mybir.dt.float32
BF16 = mybir.dt.bfloat16
assert BODY % RING == 0 and RING % CTX == 0 and B % CTX == 0


def entry(T, m):
    return m if isinstance(T, int) else T * BODY + m


def live(T, m):
    return not isinstance(T, int) or 0 <= m < B


def steps(T, m, per=1, part=None):
    part = per if part is None else part
    if isinstance(T, int):
        return 0 if m < 0 else per * m + part if m < B else per * B
    assert per * m + part > 0
    return T * (BODY * per) + (per * m + part)


def after(eng, sem, T, m, per=1, part=None):
    value = steps(T, m, per, part)
    if not isinstance(value, int) or value > 0:
        eng.wait_ge(sem, value)


def transfers(T, m, ring, per=1):
    if isinstance(T, int):
        return 0 if m < 0 else 16 * per * (m // ring + 1)
    assert m // ring + 1 > 0
    return T * (16 * per * (BODY // ring)) + 16 * per * (m // ring + 1)


def landed(eng, sems, T, m, per=1):
    value = transfers(T, m, len(sems), per)
    if not isinstance(value, int) or value > 0:
        eng.wait_ge(sems[m % len(sems)], value)


def periods(eng, period, last=B + LAG):
    for n in range(-LEAD - 1, FIRST):
        period(0, n)
    with eng.Fori(0, LOOPS) as T:
        for n in range(FIRST, FIRST + BODY):
            period(T, n)
    for n in range(LAST, last):
        period(0, n)


def build(nc, x, ctxT, W_attn, W_ffn, rows, out, part_dram):
    with ExitStack() as es:
        def sb(name, shape, dt=F32):
            return es.enter_context(nc.sbuf_tensor(name, shape, dt))

        def ps(name, shape, dt=F32):
            return es.enter_context(nc.psum_tensor(name, shape, dt))

        def sem(name):
            return es.enter_context(nc.semaphore(name))

        xs = sb("xs", [P, B, D])
        ctx_sb = sb("ctx_sb", [D, RING, P])
        x2T = sb("x2T", [D, B * P])
        w_attn = sb("w_attn", [D, 4, D])
        wq, wk, wv, wo = (w_attn[:, i] for i in range(4))
        w_ffn = sb("w_ffn", [P, 2 * FF + FC])
        w1, w2, b1_sb = w_ffn[:, 0:FF], w_ffn[:, FF:2 * FF], w_ffn[:, 2 * FF:]
        tern = sb("tern", [P, 2, FF])
        wsum = sb("wsum", [P, 2])
        wscale = sb("wscale", [P, 3, 2])
        small = sb("small", [P, 2 + 2 * D])
        gate, b_o, b2 = small[:, 0:2], small[:, 2:2 + D], small[:, 2 + D:]
        tgate = sb("tgate", [P, 2])
        gated_b_o = sb("gated_b_o", [P, D])
        ones = sb("ones", [P, P])
        ident = sb("ident", [P, P])
        identb = sb("identb", [P, P], BF16)
        mhalf = sb("mhalf", [P, 2])

        st1 = sb("st1", [P, 2, 6])
        mv = sb("mv", [P, 2, 2, 2])
        ve = sb("ve", [P, 2, 2])
        negmean = sb("negmean", [P, 2])
        rstd = sb("rstd", [P, 2, 2])
        xh = sb("xh", [P, 2, D])
        xhT = sb("xhT", [D, 2, P])
        parts = sb("parts", [P, PRING, 2, NPART, P], BF16)
        rest = sb("rest", [P, 2, 2, P])
        qa = sb("qa", [P, RING, H, P], BF16)
        ka = sb("ka", [P, RING, H, P], BF16)
        va = sb("va", [P, RING, PAIRS, VW])
        nmax = sb("nmax", [P, 2, H])
        nrest = sb("nrest", [P, 2, 2, H])
        npart = sb("npart", [P, 2, P // H, H], BF16)
        zeros = sb("zeros", [P, 2 * P])
        pairs = sb("pairs", [P, 2 * P])
        nT = sb("nT", [NPART * H, 2, P], BF16)
        probs = sb("probs", [P, 2, UNITS, QUAD * P])
        oT = sb("oT", [P, 2, 4 * P])
        rden = sb("rden", [P, 2, H])
        on = sb("on", [P, 2, D])
        onT = sb("onT", [D, 2, P])
        x2 = sb("x2", [P, 2, D])
        st2 = sb("st2", [P, 2, 6])
        xh2 = sb("xh2", [P, 2, D])
        hT = sb("hT", [P, 2, FC, GROUP * P])
        res = sb("res", [P, 2, GROUP, D])

        pS = [ps(f"pS{i}", [P, QUAD * P]) for i in range(2)]
        pT = [ps(f"pT{i}", [P, QUAD * P]) for i in range(2)]
        pO = ps("pO", [P, 4 * P])
        pR = ps("pR", [P, 4 * P])
        pA = ps("pA", [P, 4 * P])
        pB = ps("pB", [P, 4 * P])
        pAb = pA[:, P:2 * P].bitcast(BF16)

        def proj_bank(T, m):
            return pB if isinstance(T, int) and m < FILL and m % 2 else pA

        hbank = [pT[0], pS[0], pS[1], pT[1]]
        ybank = [pA, pO]

        def hidden_bank(T, g, c):
            return pA if isinstance(T, int) and g == 0 and c == 0 else hbank[c]

        x_in = [sem(f"x_in{i}") for i in range(len(XEDGES) - 1)]
        ctx_in = [sem(f"ctx_in{i}") for i in range(RING // CTX)]
        proj_in, w_in, small_in = sem("proj_in"), sem("w_in"), sem("small_in")
        parts_stored = [sem(f"parts_stored{i}") for i in range(RING)]
        aug_loaded = [sem(f"aug_loaded{i}") for i in range(RING)]
        max_loaded = [sem(f"max_loaded{i}") for i in range(2)]
        out_stored = [sem(f"out_stored{i}") for i in range(2)]
        ident_zero, ident_made, identb_made, consts_made = (
            sem("ident_zero"), sem("ident_made"), sem("identb_made"), sem("consts_made"))
        pool_pad, dve_pad, act_pad, pairs_made = sem("pool_pad"), sem("dve_pad"), sem("act_pad"), sem("pairs_made")
        va_made, pO_made = sem("va_made"), sem("pO_made")
        gates_made, gated_made, x_biased = sem("gates_made"), sem("gated_made"), sem("x_biased")
        wsum_made, wtotal_made, wstep, w_made = sem("wsum_made"), sem("wtotal_made"), sem("wstep"), sem("w_made")
        scored, keyed, pv_done = sem("scored"), sem("keyed"), sem("pv_done")
        o_turned, on_turned, wo_done = sem("o_turned"), sem("on_turned"), sem("wo_done")
        max_turned, xh_turned, xh2_turned = sem("max_turned"), sem("xh_turned"), sem("xh2_turned")
        projected, v_projected = sem("projected"), sem("v_projected")
        reduced, bn1_done, mv1_done = sem("reduced"), sem("bn1_done"), sem("mv1_done")
        xh_made, rest_made, rden_made, on_made = sem("xh_made"), sem("rest_made"), sem("rden_made"), sem("on_made")
        x2_made, bn2_done, mv2_done, stats_made = sem("x2_made"), sem("bn2_done"), sem("mv2_done"), sem("stats_made")
        exped, max_copied, o_copied, on_copied = sem("exped"), sem("max_copied"), sem("o_copied"), sem("on_copied")
        xh_copied, v_copied, first_made, x2_kept, xh2_copied = (
            sem("xh_copied"), sem("v_copied"), sem("first_made"), sem("x2_kept"), sem("xh2_copied"))
        nsplit, rstd_made, mid_made, parts_made, xh2_made = (
            sem("nsplit"), sem("rstd_made"), sem("mid_made"), sem("parts_made"), sem("xh2_made"))
        hidden, gelued, y_done, res_begun, res_made = (
            sem("hidden"), sem("gelued"), sem("y_done"), sem("res_begun"), sem("res_made"))

        def qpad_sem(m):
            return (pool_pad, m + 1) if m < RING - 1 else (act_pad, 2)

        def kpad_sem(m):
            return (dve_pad, m + 1) if m < 3 else (act_pad, (1, 3, 4)[m - 3])

        x_dram = x.rearrange("b s d -> s b d")
        out_dram = out.rearrange("(g b) s d -> g s b d", b=GROUP)
        block = es.enter_context(nc.Block())

        @block.sync
        def _(sp):
            def load_context(T, m):
                after(sp, v_projected, T, m - RING + CTX - 1)
                sp.dma_start(ctx_sb[:, m % RING:m % RING + CTX], ctxT[:, bass.ds(entry(T, m), CTX), :]
                             ).then_inc(ctx_in[m % RING // CTX], 16)

            def load_x(i):
                part = slice(XEDGES[i], XEDGES[i + 1])
                sp.dma_start(xs[:, part, :], x_dram[:, part, :]).then_inc(x_in[i], 16)

            for i in range(3):
                load_x(i)
                load_context(0, i * CTX)

            def period(T, n):
                m = n + 1
                if live(T, m):
                    after(sp, max_copied, T, m)
                    sp.dma_start(qa[MROW:MROW + NPART, m % RING], nT[:, m % 2]).then_inc(max_loaded[m % 2], 16)
                m = n + LEAD - 1
                if live(T, m):
                    after(sp, parts_made, T, m)
                    sp.dma_start(part_dram[m % RING].rearrange("w i r s -> r (w i) s"),
                                 parts[:, m % PRING].rearrange("p w i s -> p (w i) s")
                                 ).then_inc(parts_stored[m % RING], 16)
                m = n + LEAD - 2
                if live(T, m):
                    if isinstance(T, int) and m < RING:
                        sp.wait_ge(qpad_sem(m)[0], qpad_sem(m)[1])
                        sp.wait_ge(kpad_sem(m)[0], kpad_sem(m)[1])
                    landed(sp, parts_stored, T, m)
                    qsrc = part_dram[m % RING, 0].rearrange("i (k h) s -> (i k) (h s)", k=DK)
                    ksrc = part_dram[m % RING, 1].rearrange("j (k h) s -> k j (h s)", k=DK)
                    sp.dma_start(qa[0:PROD, m % RING], qsrc.unsqueeze(1).to_broadcast([NPART * DK, NPART, H * P])
                                 ).then_inc(aug_loaded[m % RING], 16)
                    for i in range(NPART):
                        rows = slice(i * NPART * DK, (i + 1) * NPART * DK)
                        sp.dma_start(ka[rows, m % RING], ksrc).then_inc(aug_loaded[m % RING], 16)
                if isinstance(T, int) and n == XLATE:
                    load_x(len(XEDGES) - 2)
                m = n + LEAD - VLAG + RING - CTX + 1
                if live(T, m) and m % CTX == 0 and m >= RING:
                    load_context(T, m)

            periods(sp, period)

            def store(T, g, entries=slice(0, GROUP), step=0):
                group = g if isinstance(T, int) else T * 2 + g
                sp.wait_ge(res_made, group + 1 + step)
                sp.dma_start(out_dram[group, :, entries], res[:, g % 2, entries]).then_inc(out_stored[g % 2], 16)

            with sp.Fori(0, GROUPS // 2 - 1) as T:
                for g in range(2):
                    store(T, g)
            store(0, GROUPS - 2)
            for i, half in enumerate(HALVES):
                store(0, GROUPS - 1, slice(half.start, half.stop), i)
            sp.wait_ge(out_stored[0], 16 * (GROUPS // 2))
            sp.wait_ge(out_stored[1], 16 * (GROUPS // 2 + 1))

        @block.gpsimd
        def _(pool):
            pool.memset(ident[:, :], 0.0).then_inc(ident_zero, 1)
            pool.wait_ge(ident_zero, 1)
            pool.affine_select(out=ident[:, :], in_=ident[:, :], compare_op=ALU.not_equal, fill=1.0, base=0,
                               pattern=[[-1, P]], channel_multiplier=1).then_inc(ident_made, 1)
            pool.memset(zeros[:, :], 0.0).then_inc(consts_made, 1)
            pool.memset(npart[:, :, :, :], 0.0).then_inc(consts_made, 1)
            pool.memset(mhalf[:, :], -0.5).then_inc(consts_made, 1)
            pool.wait_ge(consts_made, 3)

            def period(T, n):
                m, k, s = n + LEAD, n - 4, n % 2
                which = slice(0 if live(T, k) else 1, 2 if live(T, m) else 1)
                if live(T, m) or live(T, k):
                    pool.wait_ge(stats_made, T * BODY + (n + LEAD + 1))
                    if live(T, m):
                        after(pool, xh_made, T, m - 2)
                    pool.tensor_tensor(rstd[:, s, which], ve[:, 1 - s, which], mhalf[:, which], ALU.pow
                                       ).then_inc(rstd_made, 1)
                if isinstance(T, int):
                    for m in {-LEAD - 1: (0, 1), -LEAD: (2,), 1 - LEAD: (3, 4)}.get(n, ()):
                        if n > -LEAD - 1:
                            pool.wait_ge(rstd_made, n + LEAD + 1)
                        pool.memset(qa[64:P, m].rearrange("p h s -> p (h s)").bitcast(F32), 0.0).then_inc(pool_pad, 1)
                        pool.wait_ge(pool_pad, m + 1)
                m = n + 1
                if live(T, m):
                    s = m % 2
                    after(pool, reduced, T, m, UNITS)
                    after(pool, max_turned, T, m - 2)
                    pool.tensor_tensor(npart[:, s, 0], nmax[:, s], zeros[:, 0:H], ALU.add).then_inc(nsplit, 1)
                    after(pool, nsplit, T, m, 4, 1)
                    pool.tensor_tensor(nrest[:, s, 0], nmax[:, s], npart[:, s, 0], ALU.subtract).then_inc(nsplit, 1)
                    after(pool, nsplit, T, m, 4, 2)
                    pool.tensor_tensor(npart[:, s, 1], nrest[:, s, 0], zeros[:, 0:H], ALU.add).then_inc(nsplit, 1)
                    after(pool, nsplit, T, m, 4, 3)
                    pool.tensor_tensor(npart[:, s, 2], nrest[:, s, 0], npart[:, s, 1], ALU.subtract
                                       ).then_inc(nsplit, 1)
                m = n + 3
                if live(T, m):
                    if isinstance(T, int) and m == 0:
                        pool.wait_ge(gated_made, 1)
                    after(pool, xh_made, T, m)
                    pool.tensor_tensor(xs[:, entry(T, m), :], xs[:, entry(T, m), :], gated_b_o[:, :], ALU.add
                                       ).then_inc(x_biased, 1)
                if live(T, k):
                    pool.wait_ge(rstd_made, T * BODY + (n + LEAD + 1))
                m = n + LEAD - 1
                s = m % 2
                split = live(T, m) and not (isinstance(T, int) and m < DPARTS)
                if split:
                    after(pool, rest_made, T, m)
                    landed(pool, parts_stored, T, m - PRING)
                    pool.tensor_tensor(parts[:, m % PRING, :, 1], rest[:, s], zeros[:, :].rearrange("p (w s) -> p w s", w=2),
                                       ALU.add).then_inc(mid_made, 1)
                if live(T, k):
                    if isinstance(T, int):
                        after(pool, xh2_turned, T, k - 2)
                    pool.tensor_scalar(xh2[:, k % 2], x2[:, k % 2], negmean[:, 1 - n % 2:2 - n % 2],
                                       rstd[:, n % 2, 0:1], ALU.add, ALU.mult).then_inc(xh2_made, 1)
                if split:
                    after(pool, mid_made, T, m)
                    pool.tensor_tensor(parts[:, m % PRING, :, 2], rest[:, s], parts[:, m % PRING, :, 1], ALU.subtract
                                       ).then_inc(parts_made, 1)

            periods(pool, period)

        @block.scalar
        def _(act):
            act.dma_start(w_attn[:, :, :], W_attn).then_inc(proj_in, 16)
            act.dma_start(small[:, :], rows.partition_broadcast(P)).then_inc(small_in, 16)
            act.dma_start(w_ffn[:, :], W_ffn).then_inc(w_in, 16)
            act.wait_ge(small_in, 16)
            act.activation(tgate[:, :], gate, ACT.Tanh).then_inc(gates_made, 1)
            act.wait_ge(va_made, 1)

            def pad(rows, slot, value):
                dst = rows[64:P, slot].rearrange("p h s -> p (h s)").bitcast(F32).rearrange("p (a c) -> p a c", c=2 * P)
                act.copy(dst, value[64:P].unsqueeze(1).to_broadcast([P - 64, H * P // (4 * P), 2 * P])
                         ).then_inc(act_pad, 1)

            def exp(T, n, u):
                if not live(T, n):
                    return
                after(act, keyed, T, n, UNITS, u + 1)
                after(act, pv_done, T, n - 2, 2, u // 2 + 1)
                act.activation(probs[:, n % 2, u], pT[u % 2][:, :], ACT.Exp, scale=float(DK) ** -0.5
                               ).then_inc(exped, 1)

            def gelu(T, g, chunks=range(FC)):
                group = g if isinstance(T, int) else T * 2 + g
                for c in chunks:
                    act.wait_ge(hidden, group * FC + (c + 1))
                    if not isinstance(T, int) or g >= 2:
                        act.wait_ge(y_done, group - 1)
                    act.activation(hT[:, g % 2, c], hidden_bank(T, g, c)[:, :], ACT.Gelu, bias=b1_sb[:, c:c + 1]
                                   ).then_inc(gelued, 1)

            def period(T, n):
                exp(T, n - 1, 2)
                exp(T, n - 1, 3)
                if isinstance(T, int) and n == B:
                    gelu(0, 0, [0])
                m = n + LEAD
                if live(T, m):
                    if live(T, n + 1):
                        after(act, max_turned, T, n + 1)
                    else:
                        after(act, xh_turned, T, m)
                    act.copy(xhT[:, m % 2], proj_bank(T, m)[:, 0:P]).then_inc(xh_copied, 1)
                m = n + 1
                if live(T, m):
                    s = m % 2
                    after(act, max_turned, T, m)
                    landed(act, max_loaded, T, m - 2)
                    act.copy(nT[:, s], pAb[0:NPART * H, 0:P]).then_inc(max_copied, 1)
                if isinstance(T, int) and n == -LEAD:
                    act.wait_ge(pairs_made, 1)
                    pad(ka, 3, pairs)
                if isinstance(T, int) and n == -3:
                    act.wait_ge(consts_made, 3)
                    pad(qa, 5, zeros)
                if isinstance(T, int) and n in (-2, -1):
                    pad(ka, n + 6, pairs)
                m = n - 3
                if live(T, m):
                    after(act, x2_made, T, m)
                    act.copy(xs[:, entry(T, m), :], x2[:, m % 2]).then_inc(x2_kept, 1)
                m = n - 5
                if live(T, m):
                    after(act, xh2_turned, T, m)
                    e = entry(T, m)
                    act.copy(x2T[:, bass.ds(e * P, P)], pB[:, 0:P]).then_inc(xh2_copied, 1)
                exp(T, n, 0)
                m = n + LEAD
                if live(T, m - VLAG):
                    after(act, v_projected, T, m - VLAG)
                if live(T, m):
                    if m < VLAG:
                        after(act, projected, T, m)
                    stored_before(act, T, m)
                    act.copy(parts[:, m % PRING, :, 0], proj_bank(T, m)[:, 0:2 * P].rearrange("p (w s) -> p w s", w=2)
                             ).then_inc(first_made, 1)
                m = n + LEAD - VLAG
                if live(T, m):
                    after(act, pv_done, T, m - RING, 2)
                    act.copy(va[:, m % RING, :, 0:2 * DK],
                             proj_bank(T, n + LEAD)[:, 2 * P:3 * P].rearrange("p (j w) -> p j w", j=PAIRS)).then_inc(v_copied, 1)
                m = n - 2
                if live(T, m):
                    after(act, on_turned, T, m)
                    act.copy(onT[:, m % 2], pB[:, 0:P]).then_inc(on_copied, 1)
                exp(T, n, 1)
                m = n - 1
                if live(T, m):
                    after(act, pv_done, T, m, 2)
                    after(act, o_turned, T, m - 2)
                    act.copy(oT[:, m % 2], pO[:, :]).then_inc(o_copied, 1)

            def stored_before(eng, T, m):
                landed(eng, parts_stored, T, m - PRING)

            periods(act, period, OVERLAP)

            gelu(0, 0, range(1, FC))
            period(0, OVERLAP)
            gelu(0, 1)
            period(0, OVERLAP + 1)
            gelu(0, 2)
            period(0, OVERLAP + 2)
            period(0, OVERLAP + 3)
            with act.Fori(1, GROUPS // 2 - 1) as T:
                gelu(T, 1)
                gelu(T, 2)
            gelu(0, GROUPS - 1)

        @block.vector
        def _(dve):
            dve.memset(va[:, :, :, :], 1.0).then_inc(va_made, 1)
            dve.memset(pairs[:, :], TWO_ONES).then_inc(pairs_made, 1)
            dve.wait_ge(ident_made, 1)
            dve.tensor_copy(identb[:, :], ident[:, :]).then_inc(identb_made, 1)

            def weight_sums(i):
                if i == 0:
                    dve.wait_ge(w_in, 16)
                    dve.memset(ones[:, :], 1.0)
                dve.tensor_reduce(wsum[:, i:i + 1], (w1, w2)[i], AX.X, ALU.add, apply_absolute_value=True
                                  ).then_inc(wsum_made, 1)

            def weight_scales():
                dve.wait_ge(wtotal_made, 1)
                dve.tensor_scalar(wscale[:, 0], pR[:, 0:2], 1.0 / (D * FF), 1e-8, ALU.mult, ALU.max).then_inc(wstep, 1)

            def thresholds():
                dve.wait_ge(wstep, 1)
                dve.tensor_scalar(wscale[:, 1], wscale[:, 0], 0.5, None, ALU.mult).then_inc(wstep, 1)
                dve.tensor_scalar(wscale[:, 2], wscale[:, 0], -0.5, None, ALU.mult).then_inc(wstep, 1)

            def ternary(i, half):
                w, step = (w1, w2)[i], 3 + 3 * i
                if half == 0:
                    dve.wait_ge(wstep, step)
                    dve.tensor_scalar(tern[:, 0], w[:, :], wscale[:, 1, i:i + 1], None, ALU.is_gt).then_inc(wstep, 1)
                    dve.wait_ge(wstep, step + 1)
                    dve.scalar_tensor_tensor(out=tern[:, 1], in0=w[:, :], scalar=wscale[:, 2, i:i + 1],
                                             in1=tern[:, 0], op0=ALU.is_lt, op1=ALU.subtract).then_inc(wstep, 1)
                else:
                    dve.wait_ge(wstep, step + 2)
                    dve.tensor_tensor(tern[:, 0], w[:, :], tern[:, 1], ALU.add).then_inc(wstep, 1)
                    dve.wait_ge(wstep, step + 3)
                    dve.tensor_tensor(w[:, :], w[:, :], tern[:, 0], ALU.subtract).then_inc(w_made, 1)
                    dve.wait_ge(w_made, i + 1)

            def row_max(T, m, u):
                if not live(T, m):
                    return
                after(dve, scored, T, m, UNITS, u + 1)
                if u == 0:
                    after(dve, nsplit, T, m - 2, 4)
                dve.tensor_reduce(nmax[:, m % 2, u * QUAD:(u + 1) * QUAD],
                                  pS[u % 2][:, :].rearrange("p (h s) -> p h s", h=QUAD), AX.X, ALU.max,
                                  negate=True).then_inc(reduced, 1)

            def statistics(T, n):
                k, m = n - 3, n + LEAD + 1
                which = slice(0 if live(T, k) else 1, 2 if live(T, m) else 1)
                s = n % 2
                if live(T, k):
                    dve.bn_aggr(mv[:, s, 0], st2[:, k % 2]).then_inc(mv2_done, 1)
                if live(T, m):
                    dve.bn_aggr(mv[:, s, 1], st1[:, m % 2]).then_inc(mv1_done, 1)
                if live(T, k):
                    after(dve, mv2_done, T, k)
                    dve.tensor_scalar(negmean[:, s:s + 1], mv[:, s, 0, 0:1], -1.0, None, ALU.mult)
                if live(T, m):
                    after(dve, mv1_done, T, m)
                if live(T, k) or live(T, m):
                    dve.tensor_scalar(ve[:, s, which], mv[:, s, which, 1], LN_EPS, None, ALU.add).then_inc(stats_made, 1)

            def first_norm(T, n):
                m = n + LEAD
                if live(T, m):
                    dve.wait_ge(rstd_made, T * BODY + (n + LEAD + 1))
                    after(dve, xh_turned, T, m - 2)
                    dve.tensor_scalar(xh[:, m % 2], xs[:, entry(T, m), :], mv[:, (n - 1) % 2, 1, 0:1],
                                      rstd[:, n % 2, 1:2], ALU.subtract, ALU.mult).then_inc(xh_made, 1)

            def period(T, n):
                row_max(T, n + 2, 0)
                if isinstance(T, int) and n == B - LEAD:
                    thresholds()
                if not (isinstance(T, int) and n + LEAD < FILL):
                    first_norm(T, n)
                row_max(T, n + 2, 1)
                k = n - 3
                if live(T, k):
                    if isinstance(T, int) and k < 2:
                        dve.wait_ge(x_biased, k + 1)
                    after(dve, wo_done, T, k)
                    after(dve, xh2_made, T, k - 2)
                    after(dve, x2_kept, T, k - 2)
                    dve.scalar_tensor_tensor(out=x2[:, k % 2], in0=pB[:, 0:P], scalar=tgate[:, 0:1],
                                             in1=xs[:, entry(T, k), :], op0=ALU.mult, op1=ALU.add).then_inc(x2_made, 1)
                m = n + LEAD + 1
                if live(T, m):
                    if isinstance(T, int) and m in XEDGES[:-2]:
                        dve.wait_ge(x_in[XEDGES.index(m)], 16)
                    if isinstance(T, int) and n == FIRST - 1:
                        dve.wait_ge(x_in[-1], 16)
                    dve.bn_stats(st1[:, m % 2], xs[:, entry(T, m), :]).then_inc(bn1_done, 1)
                row_max(T, n + 2, 2)
                m = n - 2
                if live(T, m):
                    after(dve, o_turned, T, m)
                    den = pR[:, :].rearrange("p (b c) -> p b c", b=2)[:, :, 2 * DK:2 * P]
                    den = den.rearrange("p b (r c) -> p b r c", r=2)[:, :, :, 0:97:32]
                    dve.reciprocal(rden[:, m % 2].rearrange("p (b r j) -> p b r j", b=2, r=2), den
                                   ).then_inc(rden_made, 1)
                if live(T, k):
                    after(dve, x2_made, T, k)
                    dve.bn_stats(st2[:, k % 2], x2[:, k % 2]).then_inc(bn2_done, 1)
                if live(T, m):
                    after(dve, rden_made, T, m)
                    dve.tensor_tensor(on[:, m % 2].rearrange("p (h k) -> p h k", h=H),
                                      pR[:, :].rearrange("p (h c) -> p h c", h=H)[:, :, 0:DK],
                                      rden[:, m % 2].unsqueeze(2).to_broadcast([P, H, DK]), ALU.mult
                                      ).then_inc(on_made, 1)
                if live(T, k):
                    after(dve, bn2_done, T, k)
                if live(T, n + LEAD + 1):
                    after(dve, bn1_done, T, n + LEAD + 1)
                row_max(T, n + 2, 3)
                statistics(T, n)
                m = n + LEAD - 1
                if isinstance(T, int) and 0 <= m < DPARTS:
                    dve.wait_ge(rest_made, m + 1)
                    dve.tensor_copy(parts[:, m % PRING, :, 1], rest[:, m % 2]).then_inc(mid_made, 1)
                    dve.wait_ge(mid_made, m + 1)
                    dve.tensor_tensor(parts[:, m % PRING, :, 2], rest[:, m % 2], parts[:, m % PRING, :, 1],
                                      ALU.subtract).then_inc(parts_made, 1)
                if isinstance(T, int):
                    for m in {-LEAD - 1: (0,), -LEAD: (1, 2)}.get(n, ()):
                        dve.memset(ka[64:P, m].rearrange("p h s -> p (h s)").bitcast(F32), TWO_ONES).then_inc(dve_pad, 1)
                if isinstance(T, int) and n == 1 - LEAD:
                    dve.wait_ge(gates_made, 1)
                    dve.tensor_scalar(gated_b_o[:, :], b_o, tgate[:, 0:1], None, ALU.mult).then_inc(gated_made, 1)
                if isinstance(T, int) and n == 2 - LEAD:
                    dve.memset(pO[:, :], 0.0).then_inc(pO_made, 1)
                if isinstance(T, int) and n in (-4, -3):
                    weight_sums(n + 4)
                if isinstance(T, int) and n == -2:
                    weight_scales()
                if isinstance(T, int) and n + LEAD + 1 < FILL:
                    first_norm(T, n + 1)
                m = n + LEAD
                if live(T, m):
                    s = m % 2
                    after(dve, first_made, T, m)
                    after(dve, v_copied, T, m - VLAG)
                    after(dve, parts_made, T, m - 2)
                    dve.tensor_tensor(rest[:, s], proj_bank(T, m)[:, 0:2 * P].rearrange("p (w s) -> p w s", w=2),
                                      parts[:, m % PRING, :, 0], ALU.subtract).then_inc(rest_made, 1)
                if isinstance(T, int) and n in TERNARY:
                    ternary(*TERNARY[n])

            periods(dve, period, OVERLAP)

            def biased(T, g):
                group = g if isinstance(T, int) else T * 2 + g
                if not isinstance(T, int) or g >= 2:
                    dve.wait_ge(out_stored[g % 2], (g // 2 if isinstance(T, int) else T) * 16)
                dve.scalar_tensor_tensor(out=res[:, g % 2], in0=b2.unsqueeze(1).to_broadcast([P, GROUP, D]),
                                         scalar=tgate[:, 1:2], in1=xs[:, bass.ds(group * GROUP, GROUP), :],
                                         op0=ALU.mult, op1=ALU.add).then_inc(res_begun, 1)

            def residual(T, g, bank=None, entries=slice(0, GROUP), step=0):
                group = g if isinstance(T, int) else T * 2 + g
                bank = bank or ybank[g % 2]
                dve.wait_ge(res_begun, group + 1)
                dve.wait_ge(y_done, group + 1 + step)
                dve.scalar_tensor_tensor(out=res[:, g % 2, entries],
                                         in0=bank[:, :].rearrange("p (b d) -> p b d", b=GROUP)[:, entries],
                                         scalar=tgate[:, 1:2], in1=res[:, g % 2, entries],
                                         op0=ALU.mult, op1=ALU.add).then_inc(res_made, 1)

            period(0, OVERLAP)
            dve.wait_ge(x2_kept, 2 * GROUP)
            for g in range(2):
                biased(0, g)
            residual(0, 0)
            period(0, OVERLAP + 1)
            residual(0, 1)
            dve.wait_ge(x2_kept, B)
            with dve.Fori(1, GROUPS // 2 - 1) as T:
                for g in range(2):
                    biased(T, g)
                    residual(T, g)
            for g in (GROUPS - 2, GROUPS - 1):
                biased(0, g)
                if g == GROUPS - 2:
                    residual(0, g)
            for i, half in enumerate(HALVES):
                residual(0, GROUPS - 1, (None, pR)[i], slice(half.start, half.stop), i)

        @block.tensor
        def _(pe):
            pe.wait_ge(ident_made, 1)
            pe.wait_ge(identb_made, 1)
            pe.wait_ge(consts_made, 3)
            def keep_warm(count):
                for _ in range(count):
                    pe.matmul(pT[1][:, :], identb[:, :], zeros[:, :].bitcast(BF16), start=True, stop=True)

            def scores(T, n, u):
                if not live(T, n):
                    return
                if u == 0:
                    landed(pe, aug_loaded, T, n, 1 + NPART)
                after(pe, reduced, T, n if u >= 2 else n - 1, UNITS, (u - 2) % UNITS + 1)
                for j in range(QUAD):
                    h = u * QUAD + j
                    mm = pe.matmul(pS[u % 2][:, j * P:(j + 1) * P], qa[0:MROW, n % RING, h], ka[0:MROW, n % RING, h],
                                   start=True, stop=True)
                mm.then_inc(scored, 1)

            def keyed_scores(T, n, u):
                if not live(T, n):
                    return
                if u == 0:
                    landed(pe, max_loaded, T, n)
                after(pe, exped, T, n if u >= 2 else n - 1, UNITS, (u - 2) % UNITS + 1)
                for j in range(QUAD):
                    h = u * QUAD + j
                    mm = pe.matmul(pT[u % 2][:, j * P:(j + 1) * P], ka[:, n % RING, h], qa[:, n % RING, h],
                                   start=True, stop=True)
                mm.then_inc(keyed, 1)

            def probs_v(T, n, b):
                if not live(T, n):
                    return
                after(pe, exped, T, n, UNITS, 2 * b + 2)
                if b == 0:
                    if isinstance(T, int) and n == 0:
                        pe.wait_ge(pO_made, 1)
                    after(pe, v_copied, T, n)
                    after(pe, o_copied, T, n - 1)
                for j in range(4):
                    pr = probs[:, n % 2, 2 * b:2 * b + 2, j * P:(j + 1) * P]
                    mm = pe.matmul(pO[32 * j:32 * j + VW, b * 2 * P:(b + 1) * 2 * P].rearrange("p (r s) -> p r s", r=2),
                                   va[:, n % RING, 4 * b + j], pr, start=True, stop=True)
                mm.then_inc(pv_done, 1)

            def turn_o(T, n):
                if not live(T, n):
                    return
                after(pe, o_copied, T, n)
                after(pe, on_made, T, n - 1)
                if isinstance(T, int) and n == 0:
                    pe.wait_ge(wstep, 1)
                for b in range(2):
                    for r in range(2):
                        at = b * 2 * P + r * (P - DK)
                        mm = pe.transpose(pR[:, at:at + P], oT[:, n % 2, (2 * b + r) * P:(2 * b + r + 1) * P], ident[:, :])
                mm.then_inc(o_turned, 1)

            def turn_on(T, n):
                if not live(T, n):
                    return
                after(pe, on_made, T, n)
                after(pe, xh2_copied, T, n - 3)
                pe.transpose(pB[:, 0:P], on[:, n % 2], ident[:, :]).then_inc(on_turned, 1)

            def project_out(T, n):
                if not live(T, n):
                    return
                after(pe, on_copied, T, n)
                pe.matmul(pB[:, 0:P], onT[:, n % 2], wo[:, :], start=True, stop=True).then_inc(wo_done, 1)

            def turn_xh2(T, n):
                if not live(T, n):
                    return
                after(pe, xh2_made, T, n)
                after(pe, x2_made, T, n + 2)
                if isinstance(T, int):
                    after(pe, xh2_copied, T, n - 1)
                pe.transpose(pB[:, 0:P], xh2[:, n % 2], ident[:, :]).then_inc(xh2_turned, 1)

            def turn_max(T, n):
                if not live(T, n):
                    return
                after(pe, nsplit, T, n, 4)
                if not live(T, n + LEAD - 1):
                    after(pe, v_copied, T, n - 2 + LEAD - VLAG)
                    after(pe, rest_made, T, n - 2 + LEAD)
                pe.transpose(pAb[:, 0:P], npart[:, n % 2].rearrange("p i h -> p (i h)"), identb[:, :]
                             ).then_inc(max_turned, 1)

            def turn_xh(T, n):
                if not live(T, n):
                    return
                after(pe, xh_made, T, n)
                last = n - 2 if isinstance(T, int) and n <= FILL else n - 1
                after(pe, rest_made, T, last)
                after(pe, v_copied, T, last - VLAG)
                pe.transpose(proj_bank(T, n)[:, 0:P], xh[:, n % 2], ident[:, :]).then_inc(xh_turned, 1)

            def project(T, n):
                bank = proj_bank(T, n)
                if live(T, n):
                    after(pe, xh_copied, T, n)
                    after(pe, max_copied, T, n - LEAD + 1)
                    if n % CTX == 0:
                        pe.wait_ge(ctx_in[n % RING // CTX], T * 16 * (BODY // RING) + 16 * (n // RING + 1))
                    if isinstance(T, int) and n == 0:
                        pe.wait_ge(proj_in, 16)
                    pe.matmul(bank[:, 0:P], wq[:, :], xhT[:, n % 2], start=True, stop=True)
                    pe.matmul(bank[:, P:2 * P], wk[:, :], ctx_sb[:, n % RING], start=True, stop=True
                              ).then_inc(projected, 1)
                v = n - VLAG
                if live(T, v):
                    if not live(T, n):
                        after(pe, max_copied, T, n - LEAD + 1)
                        after(pe, v_copied, T, v - 1)
                    pe.matmul(bank[:, 2 * P:3 * P], ctx_sb[:, v % RING], wv[:, :], start=True, stop=True
                              ).then_inc(v_projected, 1)

            def up(T, g, chunks=range(FC), half=None):
                group = g if isinstance(T, int) else T * 2 + g
                first, width = (0, GROUP * P) if half is None else (half * GROUP * P // 2, GROUP * P // 2)
                for c in chunks:
                    if isinstance(T, int) and g == 0:
                        if c == 0:
                            pe.wait_ge(w_made, 1)
                            pe.wait_ge(xh2_copied, GROUP)
                            pe.wait_ge(max_copied, B)
                            pe.wait_ge(v_copied, B)
                            pe.wait_ge(rest_made, B)
                        elif c < FC - 1:
                            pe.wait_ge(reduced, B * UNITS)
                        else:
                            pe.wait_ge(exped, B * UNITS)
                            pe.wait_ge(xh2_copied, 3 * GROUP)
                    elif not isinstance(T, int) or (g, c) != (1, 0):
                        pe.wait_ge(gelued, (group - 1) * FC + (c + 1))
                    mm = pe.matmul(hidden_bank(T, g, c)[:, first:first + width], w1[:, c * P:(c + 1) * P],
                                   x2T[:, bass.ds(group * GROUP * P + first, width)], start=True, stop=True)
                    if half != 0:
                        mm.then_inc(hidden, 1)

            def period(T, n):
                scores(T, n + 2, 0)
                keyed_scores(T, n - 1, 2)
                scores(T, n + 2, 1)
                project_out(T, n - 3)
                keyed_scores(T, n - 1, 3)
                probs_v(T, n - 1, 0)
                turn_o(T, n - 2)
                if isinstance(T, int):
                    keep_warm(WARM_TURN.get(n, 0))
                turn_xh(T, n + LEAD)
                turn_max(T, n + 1)
                scores(T, n + 2, 2)
                turn_xh2(T, n - 5)
                keyed_scores(T, n, 0)
                scores(T, n + 2, 3)
                if isinstance(T, int):
                    keep_warm(WARM_BEFORE.get(n, 0))
                project(T, n + LEAD)
                if isinstance(T, int):
                    keep_warm(WARM_AFTER.get(n, 0))
                keyed_scores(T, n, 1)
                if isinstance(T, int) and n in (B - 2, B - 1):
                    up(0, 0, [0], n - B + 2)
                if isinstance(T, int) and n == B:
                    up(0, 0, [1])
                    probs_v(T, n - 1, 1)
                    up(0, 0, [2])
                    turn_on(T, n - 2)
                else:
                    turn_on(T, n - 2)
                    probs_v(T, n - 1, 1)
                if isinstance(T, int) and n == -3:
                    pe.wait_ge(wsum_made, 2)
                    pe.matmul(pR[:, 0:2], ones[:, :], wsum[:, :], start=True, stop=True).then_inc(wtotal_made, 1)

            periods(pe, period, OVERLAP)

            def down(T, g, bank=None, entries=range(GROUP)):
                group = g if isinstance(T, int) else T * 2 + g
                bank = bank or ybank[g % 2]
                pe.wait_ge(gelued, (group + 1) * FC)
                if not isinstance(T, int) or g >= 2:
                    pe.wait_ge(res_made, group - 1)
                elif g == 0:
                    pe.wait_ge(w_made, 2)
                else:
                    pe.wait_ge(o_copied, B)
                for b in entries:
                    for c in range(FC):
                        mm = pe.matmul(bank[:, b * D:(b + 1) * D], hT[:, g % 2, c, b * P:(b + 1) * P],
                                       w2[:, c * D:(c + 1) * D], start=(c == 0), stop=(c == FC - 1))
                mm.then_inc(y_done, 1)

            up(0, 0, [FC - 1])
            project_out(0, B - 2)
            turn_o(0, B - 1)
            up(0, 1, [0])
            turn_xh2(0, B - 4)
            up(0, 1, [1, 2])
            turn_on(0, B - 1)
            up(0, 1, [3])
            down(0, 0)
            project_out(0, B - 1)
            up(0, 2, [0, 1])
            turn_xh2(0, B - 3)
            up(0, 2, [2, 3])
            turn_xh2(0, B - 2)
            down(0, 1)
            turn_xh2(0, B - 1)
            pe.wait_ge(xh2_copied, B - GROUP)
            with pe.Fori(1, GROUPS // 2 - 1) as T:
                up(T, 1)
                down(T, 0)
                up(T, 2)
                down(T, 1)
            pe.wait_ge(xh2_copied, B)
            up(0, GROUPS - 1)
            down(0, GROUPS - 2)
            down(0, GROUPS - 1, entries=HALVES[0])
            down(0, GROUPS - 1, bank=pR, entries=HALVES[1])


def kernel(**inputs):
    import numpy as np
    import concourse.bacc as bacc
    from concourse.bass_utils import run_bass_kernel_spmd

    a = {k: np.asarray(v) for k, v in inputs.items()}
    W_attn = [a["L0_xattn_W_" + w].transpose(1, 2, 0).reshape(D, D) for w in "qk"]
    W_attn.append(a["L0_xattn_W_v"].reshape(2, 2, 4, D, DK).transpose(3, 0, 2, 1, 4).reshape(D, D))
    W_attn.append(a["L0_xattn_W_o"].T)
    laid = {
        "x": a["x"],
        "ctxT": a["ctx_1024"].transpose(2, 0, 1),
        "W_attn": np.stack(W_attn, 1),
        "W_ffn": np.concatenate([
            a["L0_ffn_W1"].T,
            a["L0_ffn_W2"].T.reshape(FC, P, D).transpose(1, 0, 2).reshape(P, FF),
            a["L0_ffn_b1"].reshape(FC, P).T], 1),
        "rows": np.concatenate([a["g_xattn"], a["g_ffn"], a["L0_xattn_b_o"], a["L0_ffn_b2"]]),
    }
    nc = bacc.Bacc("TRN2", target_bir_lowering=False, num_devices=1)
    arrays, aps = {}, []
    for name, v in laid.items():
        arrays[name] = np.ascontiguousarray(v)
        aps.append(nc.dram_tensor(name, arrays[name].shape, F32, kind="ExternalInput").ap())
    out = nc.dram_tensor("out", (B, P, D), F32, kind="ExternalOutput").ap()
    part_dram = nc.dram_tensor("part_dram", (RING, 2, NPART, P, P), BF16, kind="Internal").ap()
    build(nc, *aps, out, part_dram)
    r = run_bass_kernel_spmd(nc, [arrays], core_ids=[0])
    return r.results[0]["out"]
```
